# Optimizing a Trainium2 kernel written in Bass

```python
import numpy as np
import jax
import jax.numpy as jnp

def _softmax(x, axis=-1):
    return jax.nn.softmax(x, axis=axis)

def _gelu(x):
    return jax.nn.gelu(x, approximate=True)

def _silu(x):
    return jax.nn.silu(x)

def _sigmoid(x):
    return jax.nn.sigmoid(x)

def _layernorm(x, axis=-1, eps=1e-05):
    m = jnp.mean(x, axis=axis, keepdims=True)
    v = jnp.var(x, axis=axis, keepdims=True)
    return (x - m) / jnp.sqrt(v + eps)

def _scatter_add(tgt, idx, src, axis=0):
    return tgt.at[idx].add(src)

def _segment_sum(src, seg, n):
    return jax.ops.segment_sum(src, seg, n)
kernel_name = 'mk_audio_tower_d1_tok_audfeat512_r4_4482fa'

def setup_inputs(seed: int=0):
    np.random.seed(seed)
    _w = jnp.asarray

    def _rec_inputs():
        import jax
        import jax.numpy as jnp
        _rk = jax.random.key(seed)
        x = -0.000301925 + 1.00003 * jax.random.normal(jax.random.fold_in(_rk, 1), (16, 500, 80), jnp.float32)
        return x
    x = _rec_inputs()

    def _L0_tok_setup():
        import jax, jax.numpy as jnp
        import numpy as np
        B, T, F_IN = (128, 500, 80)
        F_OUT = 128
        K = 5
        DIL = 1
        EPS = 1e-05
        key = jax.random.key(seed)
        k1, k2, k3 = jax.random.split(key, 3)
        x = jax.random.normal(k1, (B, T, F_IN), dtype=jnp.float32)
        W = jax.random.normal(k2, (F_OUT, K * F_IN), dtype=jnp.float32) * 0.02
        b = jax.random.normal(k3, (F_OUT,), dtype=jnp.float32) * 0.02
        gamma = jnp.ones((F_OUT,), dtype=jnp.float32)
        beta = jnp.zeros((F_OUT,), dtype=jnp.float32)
        return {'x': x, 'W': W, 'b': b, 'gamma': gamma, 'beta': beta}
    _L0_tok_all = _L0_tok_setup()
    _L0_tok_in = {k: v for k, v in _L0_tok_all.items() if k in ('W', 'b', 'gamma', 'beta')}
    del _L0_tok_all

    def _L0_attn_setup():
        import jax, jax.numpy as jnp
        import numpy as np
        B, S, D, H, E = (8, 256, 128, 8, 64)
        key = jax.random.key(seed)
        k0, k1, k2, k3, k4 = jax.random.split(key, 5)
        x = jax.random.normal(k0, (B, S, D), dtype=jnp.float32)
        Wq = jax.random.normal(k1, (H, D, E), dtype=jnp.float32) * 0.05
        Wk = jax.random.normal(k2, (H, D, E), dtype=jnp.float32) * 0.05
        Wv = jax.random.normal(k3, (H, D, D), dtype=jnp.float32) * 0.05
        Wlt = jax.random.normal(k4, (H * D, D), dtype=jnp.float32) * 0.05
        return {'x': x, 'Wq': Wq, 'Wk': Wk, 'Wv': Wv, 'Wlt': Wlt}
    _L0_attn_all = _L0_attn_setup()
    _L0_attn_in = {k: v for k, v in _L0_attn_all.items() if k in ('Wq', 'Wk', 'Wv', 'Wlt')}
    del _L0_attn_all

    def _L0_ffn_setup():
        import jax, jax.numpy as jnp
        import numpy as np
        B, S, D, H, E = (4, 512, 128, 8, 8)
        FF = 4 * D
        HD = D // H
        EPS = 1e-05

        def _layernorm(x, g, b):
            mu = jnp.mean(x, axis=-1, keepdims=True)
            var = jnp.mean((x - mu) ** 2, axis=-1, keepdims=True)
            return (x - mu) * jax.lax.rsqrt(var + EPS) * g + b
        key = jax.random.key(seed)
        ks = jax.random.split(key, 16)
        s = 0.02
        return {'x': jax.random.normal(ks[0], (B, S, D), dtype=jnp.float32), 'ln1_g': jnp.ones((D,), jnp.float32), 'ln1_b': jnp.zeros((D,), jnp.float32), 'Wq': jax.random.normal(ks[1], (D, D), jnp.float32) * s, 'bq': jnp.zeros((D,), jnp.float32), 'Wk': jax.random.normal(ks[2], (D, D), jnp.float32) * s, 'bk': jnp.zeros((D,), jnp.float32), 'Wv': jax.random.normal(ks[3], (D, D), jnp.float32) * s, 'bv': jnp.zeros((D,), jnp.float32), 'Wo': jax.random.normal(ks[4], (D, D), jnp.float32) * s, 'bo': jnp.zeros((D,), jnp.float32), 'gate_W': jax.random.normal(ks[5], (D, E), jnp.float32) * s, 'gate_b': jnp.zeros((E,), jnp.float32), 'W1': jax.random.normal(ks[6], (E, D, FF), jnp.float32) * s, 'b1': jnp.zeros((E, FF), jnp.float32), 'W2': jax.random.normal(ks[7], (E, FF, D), jnp.float32) * s, 'b2': jnp.zeros((E, D), jnp.float32)}
    _L0_ffn_all = _L0_ffn_setup()
    _L0_ffn_in = {k: v for k, v in _L0_ffn_all.items() if k in ('ln1_g', 'ln1_b', 'Wq', 'bq', 'Wk', 'bk', 'Wv', 'bv', 'Wo', 'bo', 'gate_W', 'gate_b', 'W1', 'b1', 'W2', 'b2')}
    del _L0_ffn_all
    return {'x': x, 'L0_tok_W': _L0_tok_in['W'], 'L0_tok_b': _L0_tok_in['b'], 'L0_tok_gamma': _L0_tok_in['gamma'], 'L0_tok_beta': _L0_tok_in['beta'], 'L0_attn_Wq': _L0_attn_in['Wq'], 'L0_attn_Wk': _L0_attn_in['Wk'], 'L0_attn_Wv': _L0_attn_in['Wv'], 'L0_attn_Wlt': _L0_attn_in['Wlt'], 'L0_ffn_ln1_g': _L0_ffn_in['ln1_g'], 'L0_ffn_ln1_b': _L0_ffn_in['ln1_b'], 'L0_ffn_Wq': _L0_ffn_in['Wq'], 'L0_ffn_bq': _L0_ffn_in['bq'], 'L0_ffn_Wk': _L0_ffn_in['Wk'], 'L0_ffn_bk': _L0_ffn_in['bk'], 'L0_ffn_Wv': _L0_ffn_in['Wv'], 'L0_ffn_bv': _L0_ffn_in['bv'], 'L0_ffn_Wo': _L0_ffn_in['Wo'], 'L0_ffn_bo': _L0_ffn_in['bo'], 'L0_ffn_gate_W': _L0_ffn_in['gate_W'], 'L0_ffn_gate_b': _L0_ffn_in['gate_b'], 'L0_ffn_W1': _L0_ffn_in['W1'], 'L0_ffn_b1': _L0_ffn_in['b1'], 'L0_ffn_W2': _L0_ffn_in['W2'], 'L0_ffn_b2': _L0_ffn_in['b2']}

def reference(x, L0_tok_W, L0_tok_b, L0_tok_gamma, L0_tok_beta, L0_attn_Wq, L0_attn_Wk, L0_attn_Wv, L0_attn_Wlt, L0_ffn_ln1_g, L0_ffn_ln1_b, L0_ffn_Wq, L0_ffn_bq, L0_ffn_Wk, L0_ffn_bk, L0_ffn_Wv, L0_ffn_bv, L0_ffn_Wo, L0_ffn_bo, L0_ffn_gate_W, L0_ffn_gate_b, L0_ffn_W1, L0_ffn_b1, L0_ffn_W2, L0_ffn_b2):
    import jax
    import jax.numpy as jnp

    def _L0_tok_ref(x, W, b, gamma, beta):
        import jax, jax.numpy as jnp
        import numpy as np
        B, T, F_IN = (128, 500, 80)
        F_OUT = 128
        K = 5
        DIL = 1
        EPS = 1e-05
        Tp = T - DIL * (K - 1)
        frames = jnp.stack([x[:, i * DIL:i * DIL + Tp, :] for i in range(K)], axis=2)
        Wk = W.reshape(F_OUT, K, F_IN)
        y = jnp.einsum('btkf,okf->bto', frames, Wk) + b
        y = jax.nn.relu(y)
        mean = jnp.mean(y, axis=(0, 1))
        var = jnp.var(y, axis=(0, 1))
        y = (y - mean) * jax.lax.rsqrt(var + EPS) * gamma + beta
        return y

    def _L0_attn_ref(x, Wq, Wk, Wv, Wlt):
        import jax, jax.numpy as jnp
        import numpy as np
        B, S, D, H, E = (8, 256, 128, 8, 64)
        b, s, d = x.shape
        h, _, e = Wq.shape
        q = jnp.einsum('bsd,hde->bhse', x, Wq)
        k = jnp.einsum('bsd,hde->bhse', x, Wk)
        v = jnp.einsum('bsd,hdf->bhsf', x, Wv)
        s_a = jnp.einsum('bhie,bhje->bhij', k, q) / e
        attn = jax.nn.softmax(s_a, axis=-1)
        ax = jnp.einsum('bhtf,bhit->bhfi', v, attn)
        a_x = ax.transpose(0, 2, 1, 3).reshape(b, d, h * s)
        a_flat = a_x.reshape(-1, h * d)
        out = a_flat @ Wlt
        return out.reshape(b, s, d)

    def _L0_ffn_ref(x, ln1_g, ln1_b, Wq, bq, Wk, bk, Wv, bv, Wo, bo, gate_W, gate_b, W1, b1, W2, b2):
        import jax, jax.numpy as jnp
        import numpy as np
        B, S, D, H, E = (4, 512, 128, 8, 8)
        FF = 4 * D
        HD = D // H
        EPS = 1e-05

        def _layernorm(x, g, b):
            mu = jnp.mean(x, axis=-1, keepdims=True)
            var = jnp.mean((x - mu) ** 2, axis=-1, keepdims=True)
            return (x - mu) * jax.lax.rsqrt(var + EPS) * g + b
        b, s, d = x.shape
        q = (x @ Wq + bq).reshape(b, s, H, HD)
        k = (x @ Wk + bk).reshape(b, s, H, HD)
        v = (x @ Wv + bv).reshape(b, s, H, HD)
        scores = jnp.einsum('bqhd,bkhd->bhqk', q, k) / jnp.sqrt(jnp.float32(HD))
        attn = jax.nn.softmax(scores, axis=-1)
        o = jnp.einsum('bhqk,bkhd->bqhd', attn, v).reshape(b, s, d) @ Wo + bo
        h = _layernorm(x + o, ln1_g, ln1_b)
        t = h.reshape(b * s, d)
        probs = jax.nn.softmax(t @ gate_W + gate_b, axis=-1)
        idx = jnp.argmax(probs, axis=-1)
        gw = jnp.max(probs, axis=-1)
        hid = jax.nn.gelu(jnp.einsum('nd,edf->enf', t, W1) + b1[:, None, :])
        out_all = jnp.einsum('enf,efd->end', hid, W2) + b2[:, None, :]
        onehot = jax.nn.one_hot(idx, E, dtype=t.dtype)
        out = jnp.einsum('ne,end->nd', onehot, out_all)
        out = out * gw[:, None]
        return out.reshape(b, s, d)
    h = _L0_tok_ref(x, L0_tok_W, L0_tok_b, L0_tok_gamma, L0_tok_beta)
    h = h + _L0_attn_ref(_layernorm(h, axis=-1), L0_attn_Wq, L0_attn_Wk, L0_attn_Wv, L0_attn_Wlt)
    h = h + _L0_ffn_ref(_layernorm(h, axis=-1), L0_ffn_ln1_g, L0_ffn_ln1_b, L0_ffn_Wq, L0_ffn_bq, L0_ffn_Wk, L0_ffn_bk, L0_ffn_Wv, L0_ffn_bv, L0_ffn_Wo, L0_ffn_bo, L0_ffn_gate_W, L0_ffn_gate_b, L0_ffn_W1, L0_ffn_b1, L0_ffn_W2, L0_ffn_b2)
    return h

_drawn_inputs = setup_inputs


def setup_inputs(seed=0):
    import zlib

    import numpy as np

    out = dict(_drawn_inputs(seed))
    spreads = {'L0_tok_gamma': (1.0, 0.2),
     'L0_tok_beta': (0.0, 0.1),
     'L0_ffn_ln1_g': (1.0, 0.6),
     'L0_ffn_ln1_b': (0.0, 0.8),
     'L0_ffn_bq': (0.0, 0.8),
     'L0_ffn_bk': (0.0, 0.8),
     'L0_ffn_bv': (0.0, 0.8),
     'L0_ffn_bo': (0.0, 0.8),
     'L0_ffn_gate_b': (0.0, 0.518),
     'L0_ffn_b1': (0.0, 0.8),
     'L0_ffn_b2': (0.0, 0.487)}
    factors = {'L0_attn_Wq': 8.0,
     'L0_attn_Wk': 8.0,
     'L0_ffn_Wq': 8.0,
     'L0_ffn_Wk': 8.0,
     'L0_ffn_Wv': 8.0,
     'L0_ffn_Wo': 8.0,
     'L0_ffn_gate_W': 3.186,
     'L0_ffn_W1': 5.835,
     'L0_ffn_W2': 5.301}
    for name, (base, spread) in spreads.items():
        noise = np.random.default_rng([zlib.crc32(name.encode()), seed]).standard_normal(out[name].shape)
        drawn = base * np.exp(spread * noise) if base else spread * noise
        out[name] = jnp.asarray(drawn.astype(out[name].dtype))
    for name, factor in factors.items():
        out[name] = (out[name] * factor).astype(out[name].dtype)
    return out
```

```python
from contextlib import ExitStack

import concourse.bass as bass
import numpy as np
from concourse import mybir

ALU = mybir.AluOpType
ACT = mybir.ActivationFunctionType
AX = mybir.AxisListType
F32 = mybir.dt.float32
F32R = mybir.dt.float32r
I32 = mybir.dt.int32

B, T, FIN, D, TAPS = 16, 500, 80, 128, 5
S = T - TAPS + 1
NT = 4
R = S // NT
H1, E1 = 8, 64
H2, E2 = 8, 16
G2 = H2 // 4
NE, FF = 8, 512
NC = FF // 128
SEG = H1 * S // 128
EPS = 1e-5
RSQRT_SEED = float(0x5F3759DF)
PADW = 640

C_ID, C_BLK, C_MHI, C_MLO, C_ONE4, C_REV = 0, 128, 624, 625, 626, 632
C_END = C_REV + NT * NE

A_WQ, A_WK, A_WV, A_WLT = 0, 1024, 2048, 3072
A_END = 4096
P_WQ, P_WK, P_WV, P_WO, P_GW = 0, 256, 512, 640, 768
P_BQ, P_BK = 776, 778
P_END = 780
Q_BV, Q_BO, Q_G, Q_BETA, Q_GB, Q_B2 = 0, 128, 256, 384, 512, 520
Q_END = Q_B2 + NE * D
N_W, N_B, N_GAMMA, N_BETA = 0, TAPS * D, TAPS * D + 1, TAPS * D + 2
N_END = TAPS * D + 3
M_W1, M_W2, M_B1 = 0, NE * FF, 2 * NE * FF
M_END = 2 * NE * FF + NE * NC


def offset(h):
    return (h * S) % 128


def pieces(h):
    first = h * S // 128
    n = (offset(h) + S + 127) // 128
    return [(first + c, 128 * c, c > 0 or offset(h) == 0, c < n - 1 or (h + 1) * S % 128 == 0)
            for c in range(n)]


class Steps:

    def __init__(self, eng, sem):
        self.eng, self.sem, self.before, self.n = eng, sem, 0, 0

    def loop(self, i, per):
        self.outer, self.per = self.n, per
        self.before, self.n = i * per + self.outer, 0

    def end(self, trips):
        assert self.n == self.per, (self.n, self.per)
        self.before, self.n = 0, self.outer + trips * self.per

    def did(self, ins):
        ins.then_inc(self.sem, 1)
        self.n += 1

    def wait(self):
        self.eng.wait_ge(self.sem, self.before + self.n)


def tower(nc, xt, conv_w, att1_w, att2_w, rows_w, moe_w, consts, out):
    with ExitStack() as whole:
        def sem(name):
            return whole.enter_context(nc.semaphore(name))

        def sb(name, shape, dt=F32, ctx=whole):
            return ctx.enter_context(nc.sbuf_tensor(name, shape, dt))

        def psum(name, shape):
            return whole.enter_context(nc.psum_tensor(name, shape, F32))

        feat = sb("feat", [128, B * S])
        toks = sb("toks", [128, B * NT * D])
        xin = toks[0:FIN, 0:B * T]
        resid = toks[0:R, :].rearrange("p (b n) -> p b n", b=B)
        cst = sb("cst", [128, C_END])
        ident = cst[:, C_ID:C_ID + 128]
        mask_hi, mask_lo = cst[:, C_MHI:C_MHI + 1], cst[:, C_MLO:C_MLO + 1]
        ones4 = cst[:, C_ONE4:C_ONE4 + 1]
        moe = sb("moe", [128, M_END])
        gates = sb("gates", [R, B * NT * NE])
        gates_b = gates[:, :].rearrange("p (b n) -> p b n", b=B)
        rows = sb("rows", [R, Q_END])
        bn_st = sb("bn_st", [128, B, 6])
        bn_mv = sb("bn_mv", [128, 2])
        bn_s = sb("bn_s", [128, 4])
        ln_st = sb("ln_st", [R, NT, 6])
        ln_mv = sb("ln_mv", [R, NT, 2])
        ln_v = sb("ln_v", [128, NT])
        ln_r = sb("ln_r", [128, NT])
        ln_t = sb("ln_t", [128, NT])
        ln_out = sb("ln_out", [R, NT, D])
        mx = sb("mx", [R, NT])

        early = ExitStack()
        cw = sb("cw", [128, N_END], ctx=early)
        h1f = sb("h1f", [128, S], ctx=early)
        early.close()

        a1 = ExitStack()
        w_hi = sb("w_hi", [128, A_WLT], F32R, ctx=a1)
        w_lo = sb("w_lo", [128, A_WLT], F32R, ctx=a1)
        wlt = sb("wlt", [128, H1, D], ctx=a1)
        z_hi = sb("z_hi", [128, S], F32R, ctx=a1)
        z_lo = sb("z_lo", [128, S], F32R, ctx=a1)
        xa = sb("xa", [128, S], F32R, ctx=a1)
        xb = sb("xb", [128, S], F32R, ctx=a1)
        ya = sb("ya", [128, S], F32R, ctx=a1)
        yb = sb("yb", [128, S], F32R, ctx=a1)
        val = sb("val", [R, NT, H1, D + 1], ctx=a1)
        prob = [sb(f"prob{i}", [R, NT, PADW], ctx=a1) for i in range(2)]
        mixed = sb("mixed", [128, D * SEG], ctx=a1)
        raw = mixed[:, 0:A_WLT]
        rden = sb("rden", [128, (SEG + 2) // 3, 3], ctx=a1)
        a1.close()

        a2 = ExitStack()
        w2a = sb("w2a", [128, P_END], ctx=a2)
        v_hi = sb("v_hi", [128, P_WV], F32R, ctx=a2)
        v_lo = sb("v_lo", [128, P_WV], F32R, ctx=a2)
        zc = sb("zc", [128, S], ctx=a2)
        zc_hi = sb("zc_hi", [128, S], F32R, ctx=a2)
        zc_lo = sb("zc_lo", [128, S], F32R, ctx=a2)
        q_hi = sb("q_hi", [128, S], F32R, ctx=a2)
        q_lo = sb("q_lo", [128, S], ctx=a2)
        q_mix = sb("q_mix", [128, S], F32R, ctx=a2)
        k_lo = sb("k_lo", [128, S], ctx=a2)
        ka = [sb(f"ka{i}", [128, S], F32R, ctx=a2) for i in range(2)]
        kb = [sb(f"kb{i}", [128, S], F32R, ctx=a2) for i in range(2)]
        qa = [sb(f"qa{i}", [128, S], F32R, ctx=a2) for i in range(4)]
        qb = [sb(f"qb{i}", [128, S], F32R, ctx=a2) for i in range(4)]
        val2 = sb("val2", [R, NT, H2, 32], ctx=a2)
        prob2 = [sb(f"prob2_{i}", [R, NT, S], ctx=a2) for i in range(4)]
        o4 = sb("o4", [128, S], ctx=a2)
        rden2 = sb("rden2", [R, NT * 4], ctx=a2)
        o_tok = sb("o_tok", [R, NT, D], ctx=a2)
        o_feat = sb("o_feat", [128, S], ctx=a2)
        u = sb("u", [R, NT, D], ctx=a2)
        tc = sb("tc", [128, S], ctx=a2)
        lg = sb("lg", [R, NT, NE], ctx=a2)
        lmax = sb("lmax", [R, NT], ctx=a2)
        lexp = sb("lexp", [R, NT, NE], ctx=a2)
        lden = sb("lden", [R, NT], ctx=a2)
        pick = sb("pick", [R, NT, NE], ctx=a2)
        a2.close()

        a3 = ExitStack()
        hid = [sb(f"hid{i}", [128, NC, S], ctx=a3) for i in range(2)]
        acc = [sb(f"acc{i}", [R, NT, D], ctx=a3) for i in range(2)]
        term = [sb(f"term{i}", [R, NT, D], ctx=a3) for i in range(2)]
        gb_now = sb("gb_now", [R, NT, NE], ctx=a3)
        a3.close()

        sc = psum("sc", [128, NT, 512])
        px = psum("px", [128, 512])
        py = psum("py", [128, 512])
        po = [psum("po0", [128, 512]), psum("po1", [128, 512])]

        def tiles(bank, w=D):
            return bank[0:R, 0:NT * w].rearrange("p (t n) -> p t n", t=NT)

        d_x = [sem(f"d_x{i}") for i in range(4)]
        d_cw, d_cst, d_a1, d_a2, d_rows, d_moe = (sem(n) for n in ("d_cw", "d_cst", "d_a1", "d_a2", "d_rows", "d_moe"))
        d_out = [sem("d_out0"), sem("d_out1")]
        dve_step = sem("dve_step")
        held = sem("held")
        pool_step = sem("pool_step")
        conv_done, relu_done, stats_done, bn_ready = (sem(n) for n in ("conv_done", "relu_done", "stats_done", "bn_ready"))
        bn_applied, h1_turned, h1_kept, z1_ready, z1_turned, z1_kept = (sem(n) for n in (
            "bn_applied", "h1_turned", "h1_kept", "z1_ready", "z1_turned", "z1_kept"))
        w1_split, ones_set = sem("w1_split"), sem("ones_set")
        z_split, x_made, y_made, x_hi, y_hi, x_lo, y_lo = (sem(n) for n in (
            "z_split", "x_made", "y_made", "x_hi", "y_hi", "x_lo", "y_lo"))
        v_made, v_kept, s_made, max_done, max_turned, max_kept, st_made, exp_done = (sem(n) for n in (
            "v_made", "v_kept", "s_made", "max_done", "max_turned", "max_kept", "st_made", "exp_done"))
        pads_zero, seg_made, seg_kept, head_mixed, lt_made, h2_kept, z2_ready, z2_turned, z2_kept = (sem(n) for n in (
            "pads_zero", "seg_made", "seg_kept", "head_mixed", "lt_made", "h2_kept", "z2_ready", "z2_turned", "z2_kept"))
        w2_split, zc_split, q_made, k_made, q_hi_done, k_hi_done, q_mixed, k_mixed = (sem(n) for n in (
            "w2_split", "zc_split", "q_made", "k_made", "q_hi_done", "k_hi_done", "q_mixed", "k_mixed"))
        qab_done, v2_made, v2_kept, s2_made, max2_done, max2_turned, max2_kept = (sem(n) for n in (
            "qab_done", "v2_made", "v2_kept", "s2_made", "max2_done", "max2_turned", "max2_kept"))
        st2_made, exp2_done, o4_made, o4_kept, o4_turned, o_tok_done, of_turned, of_kept = (sem(n) for n in (
            "st2_made", "exp2_done", "o4_made", "o4_kept", "o4_turned", "o_tok_done", "of_turned", "of_kept"))
        wo_made, t_ready, t_turned, t_kept, lg_made, lsub_done, lexp_done, gates_kept, zeroed = (sem(n) for n in (
            "wo_made", "t_ready", "t_turned", "t_kept", "lg_made", "lsub_done", "lexp_done", "gates_kept", "zeroed"))
        hid_made, gelu_done, y_moe_made, y_moe_used, acc_done = (sem(n) for n in (
            "hid_made", "gelu_done", "y_moe_made", "y_moe_used", "acc_done"))

        def hold(eng):
            eng.sem_inc(held, 1)

        def feat_b(b):
            return feat[:, bass.ds(b * S, S)]

        NSEG_GROUPS = (SEG + 2) // 3
        A_PART, B_PART = 3, 4
        xw = w_hi[:, :].rearrange("p (w h n) -> p w h n", w=3, h=H1)
        xwl = w_lo[:, :].rearrange("p (w h n) -> p w h n", w=3, h=H1)

        def groups_in(h, a, b):
            return [w // 3 for w, _, _, last in pieces(h)[a:b] if last and (w % 3 == 2 or w == SEG - 1)]

        out_v = out.rearrange("b (t p) d -> p (b t) d", p=R)

        block = whole.enter_context(nc.Block())

        @block.sync
        def _(sp):
            for s in d_out:
                sp.sem_inc(s, 1)
            sp.dma_start(cw[:, :], conv_w).then_inc(d_cw, 16)
            for i in range(4):
                n = B * T // 4
                sp.dma_start(xin[:, i * n:(i + 1) * n], xt[:, i * n:(i + 1) * n]).then_inc(d_x[i], 16)
            sp.dma_start(cst[:, :], consts).then_inc(d_cst, 16)
            sp.dma_start(rows[:, :], rows_w).then_inc(d_rows, 16)
            sp.dma_start(moe[:, :], moe_w).then_inc(d_moe, 16)
            sp.wait_ge(z1_kept, 1 + B)
            sp.dma_start(raw, att1_w[:, 0:A_WLT]).then_inc(d_a1, 16)
            sp.dma_start(wlt[:, :, :].rearrange("p c n -> p (c n)"), att1_w[:, A_WLT:A_END]).then_inc(d_a1, 16)
            sp.wait_ge(z2_kept, 1 + B)
            sp.dma_start(w2a[:, :], att2_w).then_inc(d_a2, 16)
            with sp.Fori(0, B // 2) as i:
                for k in range(2):
                    sp.wait_ge(acc_done, i * 2 + k + 1)
                    sp.dma_start(out_v[:, bass.ds((i * 2 + k) * NT, NT), :], acc[k][:, :, :]).then_inc(d_out[k], 16)
            sp.wait_ge(d_out[0], 1 + 16 * B // 2)
            sp.wait_ge(d_out[1], 1 + 16 * B // 2)

        @block.tensor
        def _(pe):
            for s in (h1_turned, z1_turned, lt_made):
                pe.sem_inc(s, 1)
            pe.wait_ge(d_cw, 16)
            for i in range(4):
                pe.wait_ge(d_x[i], 16)
            with pe.Fori(0, B // 2) as i:
                for k in range(2):
                    pe.wait_ge(relu_done, 1 + i * 2)
                    bank = (px, py)[k]
                    for tap in range(TAPS):
                        mm = pe.matmul(bank[:, 0:S], cw[0:FIN, N_W + tap * D:N_W + (tap + 1) * D],
                                       xin[:, bass.ds((i * 2 + k) * T + tap, S)],
                                       start=tap == 0, stop=tap == TAPS - 1)
                    mm.then_inc(conv_done, 1)
            pe.wait_ge(d_cst, 16)
            with pe.Fori(0, B) as b:
                pe.wait_ge(bn_applied, b + 1)
                pe.wait_ge(h1_kept, 1 + b)
                for t in range(NT):
                    mm = pe.transpose(tiles(px)[:, t, :], h1f[:, t * R:(t + 1) * R], ident)
                mm.then_inc(h1_turned, 1)
                pe.wait_ge(z1_ready, b + 1)
                pe.wait_ge(z1_kept, 1 + b)
                for t in range(NT):
                    mm = pe.transpose(py[:, t * R:(t + 1) * R], ln_out[:, t, :], ident[0:R, 0:R])
                mm.then_inc(z1_turned, 1)
            pe.wait_ge(w1_split, 2)
            pe.wait_ge(ones_set, 1)

            def split_product(dst, lhs_hi, lhs_lo, rhs_hi, rhs_lo):
                pe.matmul(dst, lhs_hi, rhs_lo, start=True, stop=False)
                pe.matmul(dst, lhs_lo, rhs_hi, start=False, stop=False)
                return pe.matmul(dst, lhs_hi, rhs_hi, start=False, stop=True)

            def project(h):
                split_product(px[:, 0:S], xw[:, 0, h, :], xwl[:, 0, h, :], z_hi[:, :], z_lo[:, :]).then_inc(x_made, 1)
                split_product(py[:, 0:S], xw[:, 1, h, :], xwl[:, 1, h, :], z_hi[:, :], z_lo[:, :]).then_inc(y_made, 1)

            def values(b, i):
                t, half = i % NT, i // NT
                if i >= 2:
                    pe.wait_ge(v_kept, b * 8 + i - 1)
                w = slice(A_WV + 512 * half, A_WV + 512 * (half + 1))
                tok = slice(t * R, (t + 1) * R)
                split_product(po[i % 2][0:R, :], z_hi[:, tok], z_lo[:, tok], w_hi[:, w], w_lo[:, w]).then_inc(v_made, 1)

            def maxima(b, h):
                pe.wait_ge(x_hi, b * H1 + h + 1)
                pe.wait_ge(x_lo, b * H1 + h + 1)
                pe.wait_ge(y_hi, b * H1 + h + 1)
                pe.wait_ge(exp_done, 1 + b * H1 + h)
                for t in range(NT):
                    mm = pe.matmul(sc[0:R, t, 0:S], xa[:, t * R:(t + 1) * R], ya[:, :], start=True, stop=True)
                mm.then_inc(s_made, 1)

            def turn_max(b, h):
                pe.wait_ge(max_done, b * H1 + h + 1)
                pe.matmul(px[64:64 + NT, 0:R], mx[:, :], ident[0:R, 0:R], start=True, stop=True).then_inc(max_turned, 1)

            def scores(b, h):
                pe.wait_ge(max_kept, b * H1 + h + 1)
                pe.wait_ge(y_lo, b * H1 + h + 1)
                for t in range(NT):
                    tok = slice(t * R, (t + 1) * R)
                    pe.matmul(sc[0:R, t, 0:S], yb[0:E1 + NT, tok], xb[0:E1 + NT, :], start=True, stop=False)
                    mm = pe.matmul(sc[0:R, t, 0:S], ya[:, tok], xa[:, :], start=False, stop=True)
                mm.then_inc(st_made, 1)

            def mix(b, h, first, last):
                todo = pieces(h)
                for w, col, opens, closes in todo[first:last]:
                    bank, at = po[w // 3 % 2], w % 3 * (D + 1)
                    if opens and w % 3 == 0 and w >= 6:
                        pe.wait_ge(seg_kept, b * NSEG_GROUPS + w // 3 - 1)
                    for t in range(NT):
                        mm = pe.matmul(bank[:, at:at + D + 1], prob[h % 2][:, t, col:col + 128], val[:, t, h, :],
                                       start=opens and t == 0, stop=closes and t == NT - 1)
                    if closes and (w % 3 == 2 or w == SEG - 1):
                        mm.then_inc(seg_made, 1)

            with pe.Fori(0, B) as b:
                pe.wait_ge(z_split, b + 1)
                pe.wait_ge(h2_kept, 1 + b)
                pe.wait_ge(z2_kept, 1 + b)
                project(0)
                for i in range(4):
                    values(b, i)
                maxima(b, 0)
                for i in range(4, 8):
                    values(b, i)
                turn_max(b, 0)
                scores(b, 0)
                project(1)
                for h in range(1, H1):
                    maxima(b, h)
                    pe.wait_ge(pads_zero, b * H1 + h)
                    pe.wait_ge(v_kept, b * 8 + 8)
                    mix(b, h - 1, 0, A_PART)
                    turn_max(b, h)
                    mix(b, h - 1, A_PART, B_PART)
                    scores(b, h)
                    if h < H1 - 1:
                        project(h + 1)
                    mix(b, h - 1, B_PART, 9)
                pe.wait_ge(exp_done, 1 + (b + 1) * H1)
                pe.wait_ge(pads_zero, (b + 1) * H1)
                mix(b, H1 - 1, 0, 9)
                pe.wait_ge(seg_kept, (b + 1) * NSEG_GROUPS)
                for t in range(NT):
                    for c in range(H1):
                        a = H1 * R * t + c
                        mm = pe.matmul(tiles(px)[:, t, :], mixed[:, a:a + H1 * (R - 1) + 1:H1], wlt[:, c, :],
                                       start=c == 0, stop=c == H1 - 1)
                mm.then_inc(lt_made, 1)
                pe.wait_ge(z2_ready, b + 1)
                for t in range(NT):
                    mm = pe.transpose(py[:, t * R:(t + 1) * R], ln_out[:, t, :], ident[0:R, 0:R])
                mm.then_inc(z2_turned, 1)

            pe.wait_ge(w2_split, 2)
            pe.wait_ge(zeroed, 10)
            with pe.Fori(0, B) as b:
                pe.wait_ge(zc_split, b + 1)
                pe.wait_ge(t_kept, 1 + b)
                pe.wait_ge(gates_kept, 1 + b)
                for t in range(NT):
                    mm = pe.matmul(tiles(po[1])[:, t, :], zc[:, t * R:(t + 1) * R], w2a[:, P_WV:P_WV + D],
                                   start=True, stop=True)
                mm.then_inc(v2_made, 1)
                for g in range(G2):
                    if g:
                        pe.wait_ge(q_mixed, b * G2 + g)
                        pe.wait_ge(k_mixed, b * G2 + g)
                        pe.wait_ge(o_tok_done, b * G2 + g)
                    split_product(px[:, 0:S], v_hi[:, P_WQ + 128 * g:P_WQ + 128 * (g + 1)], v_lo[:, P_WQ + 128 * g:P_WQ + 128 * (g + 1)],
                                  zc_hi[:, :], zc_lo[:, :]).then_inc(q_made, 1)
                    split_product(py[:, 0:S], v_hi[:, P_WK + 128 * g:P_WK + 128 * (g + 1)], v_lo[:, P_WK + 128 * g:P_WK + 128 * (g + 1)],
                                  zc_hi[:, :], zc_lo[:, :]).then_inc(k_made, 1)
                    for j in range(4):
                        n = b * H2 + 4 * g + j
                        pe.wait_ge(qab_done, n + 1)
                        pe.wait_ge(k_mixed, b * G2 + g + 1)
                        pe.wait_ge(exp2_done, 1 + n)
                        for t in range(NT):
                            mm = pe.matmul(sc[0:R, t, 0:S], qa[j][:, t * R:(t + 1) * R], ka[g][:, :], start=True, stop=True)
                        mm.then_inc(s2_made, 1)
                        pe.wait_ge(max2_done, n + 1)
                        if g == 0 and j == 0:
                            pe.wait_ge(v2_kept, b + 1)
                        pe.matmul(po[1][32 * j:32 * j + NT, 0:R], mx[:, :], ident[0:R, 0:R], start=True, stop=True,
                                  tile_position=(0, 32 * j)).then_inc(max2_turned, 1)
                        pe.wait_ge(max2_kept, n + 1)
                        for t in range(NT):
                            tok = slice(t * R, (t + 1) * R)
                            pe.matmul(sc[0:R, t, 0:S], kb[g][:, tok], qb[j][:, :], start=True, stop=False)
                            mm = pe.matmul(sc[0:R, t, 0:S], ka[g][:, tok], qa[j][:, :], start=False, stop=True)
                        mm.then_inc(st2_made, 1)
                    pe.wait_ge(exp2_done, 1 + b * H2 + 4 * g + 4)
                    pe.wait_ge(v2_kept, b + 1)
                    pe.wait_ge(o4_kept, 1 + b * G2 + g)
                    for t in range(NT):
                        for j in range(4):
                            mm = pe.matmul(po[0][32 * j:32 * j + 32, 0:S], val2[:, t, 4 * g + j, :], prob2[j][:, t, :],
                                           start=t == 0, stop=t == NT - 1, tile_position=(0, 32 * j))
                    mm.then_inc(o4_made, 1)
                    pe.wait_ge(o4_kept, 1 + b * G2 + g + 1)
                    for t in range(NT):
                        mm = pe.transpose(tiles(px)[:, t, :], o4[:, t * R:(t + 1) * R], ident)
                    mm.then_inc(o4_turned, 1)
                pe.wait_ge(o_tok_done, b * G2 + G2)
                for t in range(NT):
                    mm = pe.transpose(py[:, t * R:(t + 1) * R], o_tok[:, t, :], ident[0:R, 0:R])
                mm.then_inc(of_turned, 1)
                pe.wait_ge(of_kept, b + 1)
                for t in range(NT):
                    tok = slice(t * R, (t + 1) * R)
                    pe.matmul(tiles(px)[:, t, :], zc[:, tok], ident, start=True, stop=False)
                    mm = pe.matmul(tiles(px)[:, t, :], o_feat[:, tok], w2a[:, P_WO:P_WO + D], start=False, stop=True)
                mm.then_inc(wo_made, 1)
                pe.wait_ge(t_ready, b + 1)
                for t in range(NT):
                    mm = pe.transpose(py[:, t * R:(t + 1) * R], ln_out[:, t, :], ident[0:R, 0:R])
                mm.then_inc(t_turned, 1)
                pe.wait_ge(t_kept, 1 + b + 1)
                for t in range(NT):
                    mm = pe.matmul(tiles(px, NE)[:, t, :], tc[:, t * R:(t + 1) * R], w2a[:, P_GW:P_GW + NE],
                                   start=True, stop=True)
                mm.then_inc(lg_made, 1)

            pe.wait_ge(d_moe, 16)
            pe.wait_ge(gates_kept, 1 + B)
            w1 = moe[:, M_W1:M_W2].rearrange("p (e n) -> p e n", e=NE)
            w2 = moe[:, M_W2:M_B1].rearrange("p (e c n) -> p e c n", e=NE, c=NC)

            def up(b, e):
                for c in range(NC):
                    pe.wait_ge(gelu_done, 1 + ((b * NE + e) * NC + c - (NC - 1) if e else b * NE * NC))
                    pe.matmul(sc[:, c, 0:S], w1[:, e, c * 128:(c + 1) * 128], feat_b(b), start=True, stop=True).then_inc(hid_made, 1)

            def down(b, e):
                pe.wait_ge(gelu_done, 1 + (b * NE + e + 1) * NC)
                if e >= 2:
                    pe.wait_ge(y_moe_used, 1 + b * NE + e - 1)
                else:
                    pe.wait_ge(y_moe_used, 1 + b * NE)
                for t in range(NT):
                    for c in range(NC):
                        mm = pe.matmul(tiles(po[e % 2])[:, t, :], hid[e % 2][:, c, t * R:(t + 1) * R], w2[:, e, c, :],
                                       start=c == 0, stop=c == NC - 1)
                mm.then_inc(y_moe_made, 1)

            with pe.Fori(0, B) as b:
                up(b, 0)
                for e in range(1, NE):
                    up(b, e)
                    down(b, e - 1)
                down(b, NE - 1)

        @block.scalar
        def _(act):
            for s in (relu_done, h1_kept, z1_kept, exp_done, z2_kept, t_kept, o4_kept, exp2_done, gelu_done):
                act.sem_inc(s, 1)
            act.wait_ge(d_cw, 16)
            act.wait_ge(d_cst, 16)
            with act.Fori(0, B // 2) as i:
                for k, bank in enumerate((px, py)):
                    act.wait_ge(conv_done, i * 2 + k + 1)
                    act.activation(feat_b(i * 2 + k), bank[:, 0:S], ACT.Relu, bias=cw[:, N_B:N_B + 1]).then_inc(relu_done, 1)
            act.wait_ge(bn_ready, 1)
            with act.Fori(0, B) as b:
                act.wait_ge(h1_turned, 1 + b)
                act.activation(h1f[:, :], feat_b(b), ACT.Identity, bias=bn_s[:, 3:4], scale=bn_s[:, 2:3]).then_inc(bn_applied, 1)
                act.wait_ge(h1_turned, 1 + b + 1)
                hold(act)
                act.copy(resid[:, bass.ds(b, 1), :].rearrange("p a n -> p (a n)"), px[0:R, :]).then_inc(h1_kept, 1)
                act.wait_ge(z1_turned, 1 + b + 1)
                hold(act)
                act.copy(feat_b(b), py[:, 0:S]).then_inc(z1_kept, 1)

            def high_parts(b, h):
                act.wait_ge(x_made, b * H1 + h + 1)
                act.copy(xb[:, :], px[:, 0:S])
                act.copy(xa[0:E1, :], px[0:E1, 0:S]).then_inc(x_hi, 1)
                act.wait_ge(y_made, b * H1 + h + 1)
                act.copy(ya[:, :], py[:, 0:S]).then_inc(y_hi, 1)

            with act.Fori(0, B) as b:
                high_parts(b, 0)
                for i in range(8):
                    act.wait_ge(v_made, b * 8 + i + 1)
                    t, half = i % NT, i // NT
                    act.copy(val[:, t, 4 * half:4 * half + 4, 0:D],
                             po[i % 2][0:R, :].rearrange("p (h n) -> p h n", h=4)).then_inc(v_kept, 1)
                for h in range(H1):
                    act.wait_ge(st_made, b * H1 + h + 1)
                    act.activation(prob[h % 2][:, :, offset(h):offset(h) + S], sc[0:R, :, 0:S], ACT.Exp,
                                   scale=1.0 / E1).then_inc(exp_done, 1)
                    if h < H1 - 1:
                        high_parts(b, h + 1)
                act.wait_ge(z2_turned, b + 1)
                hold(act)
                act.copy(feat_b(b), py[:, 0:S]).then_inc(z2_kept, 1)

            act.wait_ge(d_a2, 16)
            act.wait_ge(zeroed, 10)
            with act.Fori(0, B) as b:
                for g in range(G2):
                    act.wait_ge(q_made, b * G2 + g + 1)
                    act.activation(q_hi[:, :], px[:, 0:S], ACT.Identity, bias=w2a[:, P_BQ + g:P_BQ + g + 1]).then_inc(q_hi_done, 1)
                    act.wait_ge(k_made, b * G2 + g + 1)
                    act.activation(ka[g][:, :], py[:, 0:S], ACT.Identity, bias=w2a[:, P_BK + g:P_BK + g + 1]).then_inc(k_hi_done, 1)
                    act.wait_ge(q_hi_done, b * G2 + g + 1)
                    act.wait_ge(q_mixed, b * G2 + g + 1)
                    for j in range(4):
                        rows_j = slice(32 * j, 32 * j + 32)
                        act.copy(qb[j][rows_j, :], q_hi[rows_j, :].bitcast(F32))
                        act.copy(qa[j][rows_j, :], q_mix[rows_j, :].bitcast(F32)).then_inc(qab_done, 1)
                    for j in range(4):
                        act.wait_ge(st2_made, b * H2 + 4 * g + j + 1)
                        act.activation(prob2[j][:, :, :], sc[0:R, :, 0:S], ACT.Exp, scale=float(E2) ** -0.5).then_inc(exp2_done, 1)
                    act.wait_ge(o4_made, b * G2 + g + 1)
                    act.copy(o4[:, :], po[0][:, 0:S]).then_inc(o4_kept, 1)
                act.wait_ge(of_turned, b + 1)
                act.copy(o_feat[:, :], py[:, 0:S]).then_inc(of_kept, 1)
                act.wait_ge(t_turned, b + 1)
                hold(act)
                act.copy(feat_b(b), py[:, 0:S])
                act.copy(tc[:, :], py[:, 0:S]).then_inc(t_kept, 1)
                act.wait_ge(lsub_done, b + 1)
                act.activation(lexp[:, :, :], lg[:, :, :], ACT.Exp).then_inc(lexp_done, 1)

            b1 = moe[:, M_B1:M_END]
            act.wait_ge(d_moe, 16)
            with act.Fori(0, B) as b:
                for e in range(NE):
                    if e >= 2:
                        act.wait_ge(y_moe_made, b * NE + e - 1)
                    for c in range(NC):
                        act.wait_ge(hid_made, (b * NE + e) * NC + c + 1)
                        act.activation(hid[e % 2][:, c, :], sc[:, c, 0:S], ACT.Gelu_apprx_tanh,
                                       bias=b1[:, e * NC + c:e * NC + c + 1]).then_inc(gelu_done, 1)

        @block.vector
        def _(dve):
            for s in (h2_kept, gates_kept, y_moe_used):
                dve.sem_inc(s, 1)
            step = Steps(dve, dve_step)

            def rsqrt(out_, var, scratch, v):
                step.did(dve.tensor_scalar(v, var, EPS, None, ALU.add))
                step.wait()
                step.did(dve.tensor_scalar(out_.bitcast(I32), v.bitcast(I32), -0.5, RSQRT_SEED, ALU.mult, ALU.add))
                step.wait()
                for _ in range(3):
                    step.did(dve.scalar_tensor_tensor(out=scratch, in0=out_, scalar=-0.5, in1=out_, op0=ALU.mult, op1=ALU.mult))
                    step.wait()
                    step.did(dve.tensor_tensor(scratch, scratch, v, ALU.mult))
                    step.wait()
                    step.did(dve.scalar_tensor_tensor(out=out_, in0=scratch, scalar=1.5, in1=out_, op0=ALU.add, op1=ALU.mult))
                    step.wait()

            def layer_norm(src):
                hold(dve)
                for t in range(NT):
                    st = dve.bn_stats(ln_st[:, t, :], src[:, t, :])
                step.did(st)
                step.wait()
                hold(dve)
                for t in range(NT):
                    st = dve.bn_aggr(ln_mv[:, t, :], ln_st[:, t, :])
                step.did(st)
                step.wait()
                rsqrt(ln_r[0:R, :], ln_mv[:, :, 1], ln_t[0:R, :], ln_v[0:R, :])
                for t in range(NT):
                    last = dve.tensor_scalar(ln_out[:, t, :], src[:, t, :], ln_mv[:, t, 0:1], ln_r[0:R, t:t + 1],
                                             ALU.subtract, ALU.mult)
                return last

            LN_STEPS = 13

            dve.wait_ge(d_cst, 16)
            with dve.Fori(0, B) as b:
                dve.wait_ge(relu_done, 1 + b + 1)
                hold(dve)
                dve.bn_stats(bn_st[:, bass.ds(b, 1), :].rearrange("p a n -> p (a n)"), feat_b(b)).then_inc(stats_done, 1)
            dve.wait_ge(stats_done, B)
            step.did(dve.bn_aggr(bn_mv[:, :], bn_st[:, :, :]))
            step.wait()
            rsqrt(bn_s[:, 0:1], bn_mv[:, 1:2], bn_s[:, 1:2], ln_v[:, 0:1])
            dve.wait_ge(d_cw, 16)
            step.did(dve.tensor_tensor(bn_s[:, 2:3], bn_s[:, 0:1], cw[:, N_GAMMA:N_GAMMA + 1], ALU.mult))
            step.wait()
            step.did(dve.tensor_tensor(bn_s[:, 1:2], bn_s[:, 2:3], bn_mv[:, 0:1], ALU.mult))
            step.wait()
            dve.tensor_tensor(bn_s[:, 3:4], cw[:, N_BETA:N_BETA + 1], bn_s[:, 1:2], ALU.subtract).then_inc(bn_ready, 1)

            with dve.Fori(0, B) as b:
                step.loop(b, LN_STEPS)
                dve.wait_ge(h1_kept, 1 + b + 1)
                dve.wait_ge(z1_turned, 1 + b)
                layer_norm(resid[:, bass.ds(b, 1), :].rearrange("p a (t n) -> p (a t) n", t=NT)).then_inc(z1_ready, 1)
                step.end(B)

            dve.wait_ge(d_a1, 32)
            step.did(dve.tensor_copy(w_hi[:, :], raw))
            step.wait()
            dve.tensor_tensor(w_lo[:, :], raw, w_hi[:, :].bitcast(F32), ALU.subtract).then_inc(w1_split, 2)

            def low_parts(b, h):
                dve.wait_ge(x_hi, b * H1 + h + 1)
                dve.tensor_tensor(xa[E1:128, :], px[E1:128, 0:S], xb[E1:128, :].bitcast(F32), ALU.subtract).then_inc(x_lo, 1)
                dve.wait_ge(y_hi, b * H1 + h + 1)
                dve.tensor_tensor(yb[0:E1, :], py[0:E1, 0:S], ya[0:E1, :].bitcast(F32), ALU.subtract).then_inc(y_lo, 1)

            def keep_group(b, q):
                n = min(3, SEG - 3 * q)
                src = po[q % 2][:, 0:n * (D + 1)].rearrange("p (j n) -> p j n", j=n)
                dve.wait_ge(seg_made, b * NSEG_GROUPS + q + 1)
                step.did(dve.reciprocal(rden[:, q, 0:n], src[:, :, D]))
                step.wait()
                dst = mixed[:, :].rearrange("p (f w) -> p w f", w=SEG)[:, 3 * q:3 * q + n, :]
                dve.tensor_tensor(dst, src[:, :, 0:D], rden[:, q, 0:n].unsqueeze(2).broadcast_to([128, n, D]),
                                  ALU.mult).then_inc(seg_kept, 1)

            def keep_max(rows_, bank, dst, b_h, turned, kept):
                dve.wait_ge(turned, b_h + 1)
                dve.tensor_tensor(dst[rows_, :].rearrange("p (t n) -> p t n", t=NT),
                                  bank[rows_, 0:R].unsqueeze(1).broadcast_to([NT, NT, R]),
                                  cst[rows_, C_BLK:C_BLK + S].rearrange("p (t n) -> p t n", t=NT),
                                  ALU.mult).then_inc(kept, 1)

            with dve.Fori(0, B) as b:
                step.loop(b, 1 + NSEG_GROUPS + LN_STEPS)
                step.did(dve.tensor_copy(z_hi[:, :], feat_b(b)))
                step.wait()
                dve.tensor_tensor(z_lo[:, :], feat_b(b), z_hi[:, :].bitcast(F32), ALU.subtract).then_inc(z_split, 1)
                low_parts(b, 0)
                for h in range(H1):
                    dve.wait_ge(s_made, b * H1 + h + 1)
                    dve.tensor_reduce(mx[:, :], sc[0:R, :, 0:S], AX.X, ALU.max).then_inc(max_done, 1)
                    keep_max(slice(64, 64 + NT), px, xb, b * H1 + h, max_turned, max_kept)
                    if h:
                        for q in groups_in(h - 1, 0, B_PART):
                            keep_group(b, q)
                    if h < H1 - 1:
                        low_parts(b, h + 1)
                    if h:
                        for q in groups_in(h - 1, B_PART, 9):
                            keep_group(b, q)
                for q in groups_in(H1 - 1, 0, 9):
                    keep_group(b, q)
                rb = resid[:, bass.ds(b, 1), :].rearrange("p a n -> p (a n)")
                dve.wait_ge(lt_made, 1 + b + 1)
                dve.tensor_tensor(rb, rb, px[0:R, :], ALU.add).then_inc(h2_kept, 1)
                dve.wait_ge(h2_kept, 1 + b + 1)
                layer_norm(resid[:, bass.ds(b, 1), :].rearrange("p a (t n) -> p (a t) n", t=NT)).then_inc(z2_ready, 1)
                step.end(B)

            dve.wait_ge(d_a2, 16)
            dve.wait_ge(d_rows, 16)
            step.did(dve.tensor_copy(v_hi[:, :], w2a[:, 0:P_WV]))
            step.wait()
            dve.tensor_tensor(v_lo[:, :], w2a[:, 0:P_WV], v_hi[:, :].bitcast(F32), ALU.subtract).then_inc(w2_split, 2)
            dve.wait_ge(zeroed, 10)

            def row(c, n=D):
                return rows[:, c:c + n].unsqueeze(1).broadcast_to([R, NT, n])

            with dve.Fori(0, B) as b:
                step.loop(b, 1 + 4 * G2 + 1 + LN_STEPS + 2 + 6)
                dve.tensor_copy(zc[:, :], feat_b(b))
                step.did(dve.tensor_copy(zc_hi[:, :], feat_b(b)))
                step.wait()
                dve.tensor_tensor(zc_lo[:, :], feat_b(b), zc_hi[:, :].bitcast(F32), ALU.subtract).then_inc(zc_split, 1)
                dve.wait_ge(v2_made, b + 1)
                dve.tensor_tensor(val2[:, :, :, 0:E2],
                                  tiles(po[1]).rearrange("p t (h n) -> p t h n", h=H2),
                                  rows[:, Q_BV:Q_BV + D].rearrange("p (h n) -> p h n", h=H2).unsqueeze(1).broadcast_to([R, NT, H2, E2]),
                                  ALU.add).then_inc(v2_kept, 1)
                for g in range(G2):
                    dve.wait_ge(q_hi_done, b * G2 + g + 1)
                    step.did(dve.scalar_tensor_tensor(out=q_lo[:, :], in0=px[:, 0:S], scalar=w2a[:, P_BQ + g:P_BQ + g + 1],
                                                      in1=q_hi[:, :].bitcast(F32), op0=ALU.add, op1=ALU.subtract))
                    dve.wait_ge(k_hi_done, b * G2 + g + 1)
                    step.did(dve.scalar_tensor_tensor(out=k_lo[:, :], in0=py[:, 0:S], scalar=w2a[:, P_BK + g:P_BK + g + 1],
                                                      in1=ka[g][:, :].bitcast(F32), op0=ALU.add, op1=ALU.subtract))
                    step.wait()
                    step.did(dve.tensor_scalar(q_lo[:, :], q_lo[:, :], mask_lo, None, ALU.mult))
                    dve.tensor_scalar(kb[g][:, :], k_lo[:, :], mask_lo, ones4, ALU.mult, ALU.add).then_inc(k_mixed, 1)
                    step.wait()
                    dve.scalar_tensor_tensor(out=q_mix[:, :], in0=q_hi[:, :].bitcast(F32), scalar=mask_hi, in1=q_lo[:, :],
                                             op0=ALU.mult, op1=ALU.add).then_inc(q_mixed, 1)
                    for j in range(4):
                        n = b * H2 + 4 * g + j
                        dve.wait_ge(s2_made, n + 1)
                        dve.tensor_reduce(mx[:, :], sc[0:R, :, 0:S], AX.X, ALU.max).then_inc(max2_done, 1)
                        keep_max(slice(32 * j, 32 * j + NT), po[1], qb[j], n, max2_turned, max2_kept)
                    dve.wait_ge(o4_turned, b * G2 + g + 1)
                    o_in = tiles(px).rearrange("p t (j n) -> p t j n", j=4)
                    step.did(dve.reciprocal(rden2[:, :].rearrange("p (t j) -> p t j", t=NT), o_in[:, :, :, E2]))
                    step.wait()
                    dve.tensor_tensor(o_tok[:, :, 64 * g:64 * (g + 1)].rearrange("p t (j n) -> p t j n", j=4),
                                      o_in[:, :, :, 0:E2],
                                      rden2[:, :].rearrange("p (t j) -> p t j", t=NT).unsqueeze(3).broadcast_to([R, NT, 4, E2]),
                                      ALU.mult).then_inc(o_tok_done, 1)
                dve.wait_ge(wo_made, b + 1)
                step.did(dve.tensor_tensor(u[:, :, :], tiles(px), row(Q_BO), ALU.add))
                step.wait()
                step.did(layer_norm(u))
                step.wait()
                step.did(dve.tensor_tensor(ln_out[:, :, :], ln_out[:, :, :], row(Q_G), ALU.mult))
                step.wait()
                dve.tensor_tensor(ln_out[:, :, :], ln_out[:, :, :], row(Q_BETA), ALU.add).then_inc(t_ready, 1)
                dve.wait_ge(lg_made, b + 1)
                step.did(dve.tensor_tensor(lg[:, :, :], tiles(px, NE), row(Q_GB, NE), ALU.add))
                step.wait()
                step.did(dve.tensor_reduce(lmax[:, :], lg[:, :, :], AX.X, ALU.max))
                step.wait()
                many = lambda a: a.unsqueeze(2).broadcast_to([R, NT, NE])
                rev = cst[0:R, C_REV:C_REV + NT * NE].rearrange("p (t n) -> p t n", t=NT)
                dve.tensor_tensor(lg[:, :, :], lg[:, :, :], many(lmax[:, :]), ALU.subtract).then_inc(lsub_done, 1)
                dve.wait_ge(lsub_done, b + 1)
                step.did(dve.scalar_tensor_tensor(out=pick[:, :, :], in0=lg[:, :, :], scalar=0.0, in1=rev, op0=ALU.is_equal, op1=ALU.mult))
                step.wait()
                step.did(dve.tensor_reduce(lmax[:, :], pick[:, :, :], AX.X, ALU.max))
                dve.wait_ge(lexp_done, b + 1)
                step.did(dve.tensor_reduce(lden[:, :], lexp[:, :, :], AX.X, ALU.add))
                step.wait()
                dve.tensor_tensor(pick[:, :, :], pick[:, :, :], many(lmax[:, :]), ALU.is_equal)
                step.did(dve.reciprocal(lden[:, :], lden[:, :]))
                step.wait()
                dve.tensor_tensor(gates_b[:, bass.ds(b, 1), :].rearrange("p a (t n) -> p (a t) n", t=NT), pick[:, :, :],
                                  many(lden[:, :]), ALU.mult).then_inc(gates_kept, 1)
                step.end(B)

            dve.wait_ge(gates_kept, 1 + B)
            with dve.Fori(0, B // 2) as i:
                step.loop(i, 2 * 2 * NE)
                for k in range(2):
                    b = i * 2 + k
                    step.did(dve.tensor_copy(gb_now[:, :, :], gates_b[:, bass.ds(b, 1), :].rearrange("p a (t n) -> p (a t) n", t=NT)))
                    dve.wait_ge(d_out[k], 1 + i * 16)
                    for e in range(NE):
                        dve.wait_ge(y_moe_made, b * NE + e + 1)
                        dve.tensor_tensor(term[e % 2][:, :, :], tiles(po[e % 2]), row(Q_B2 + e * D), ALU.add).then_inc(y_moe_used, 1)
                        dve.wait_ge(y_moe_used, 1 + b * NE + e + 1)
                        step.wait()
                        step.did(dve.tensor_tensor(term[e % 2][:, :, :], term[e % 2][:, :, :],
                                                   gb_now[:, :, e:e + 1].broadcast_to([R, NT, D]), ALU.mult))
                        step.wait()
                        if e == 0:
                            other = resid[:, bass.ds(b, 1), :].rearrange("p a (t n) -> p (a t) n", t=NT)
                        else:
                            other = acc[k][:, :, :]
                        last = dve.tensor_tensor(acc[k][:, :, :], other, term[e % 2][:, :, :], ALU.add)
                        if e == NE - 1:
                            last.then_inc(acc_done, 1)
                        else:
                            step.did(last)
                step.end(B // 2)

        @block.gpsimd
        def _(pool):
            step = Steps(pool, pool_step)

            def fill(dst, value):
                step.wait()
                hold(pool)
                step.did(pool.memset(dst, value))

            pool.wait_ge(z1_kept, 1 + B)
            fill(yb[E1:E1 + 32, :].bitcast(F32), 1.0)
            fill(val[:, :, :, D:D + 1], 1.0)
            step.wait()
            pool.sem_inc(ones_set, 1)
            pads = [[(0, offset(h)), (offset(h) + S, (offset(h) + S + 127) // 128 * 128)] for h in range(H1)]
            with pool.Fori(0, B) as b:
                step.loop(b, sum(hi > lo for h in range(H1) for lo, hi in pads[h]))
                for h in range(H1):
                    if h < 2:
                        pool.wait_ge(lt_made, 1 + b)
                    else:
                        pool.wait_ge(max_turned, b * H1 + h + 1)
                    hold(pool)
                    for lo, hi in pads[h]:
                        if hi > lo:
                            fill(prob[h % 2][:, :, lo:hi], 0.0)
                    step.wait()
                    pool.sem_inc(pads_zero, 1)
                step.end(B)
            pool.wait_ge(z2_kept, 1 + B)
            for j in range(4):
                fill(qa[j][:, :].bitcast(F32), 0.0)
                fill(qb[j][:, :].bitcast(F32), 0.0)
            fill(o_tok[:, :, :], 0.0)
            fill(val2[:, :, :, E2:32], 1.0)
            step.wait()
            pool.sem_inc(zeroed, 10)


_IN = ("xt", "conv_w", "att1_w", "att2_w", "rows_w", "moe_w", "consts")


def kernel(**inputs):
    import concourse.bacc as _bacc
    from concourse.bass_utils import run_bass_kernel_spmd as _run

    a = {k: np.asarray(v) for k, v in inputs.items()}
    f32 = np.float32

    def wide(w, n):
        full = np.zeros((128, w.shape[1]), f32)
        full[:n] = w
        return full

    arrays = {}
    arrays["xt"] = np.ascontiguousarray(a["x"].transpose(2, 0, 1).reshape(FIN, B * T))
    w = a["L0_tok_W"].reshape(D, TAPS, FIN).transpose(2, 1, 0).reshape(FIN, TAPS * D)
    arrays["conv_w"] = np.concatenate([wide(w, FIN), a["L0_tok_b"][:, None], a["L0_tok_gamma"][:, None],
                                       a["L0_tok_beta"][:, None]], axis=1)

    def twice(w):
        w = w.transpose(1, 0, 2)
        return np.concatenate([w, w], axis=2).reshape(D, -1)

    arrays["att1_w"] = np.concatenate([
        twice(a["L0_attn_Wk"]), twice(a["L0_attn_Wq"]), a["L0_attn_Wv"].transpose(1, 0, 2).reshape(D, -1),
        a["L0_attn_Wlt"].reshape(H1, 128, D).transpose(1, 0, 2).reshape(128, -1)], axis=1)

    cols = np.array([[16 * (4 * g + p // 32) + p % 16 for p in range(128)] for g in range(G2)])
    arrays["att2_w"] = np.concatenate([
        a["L0_ffn_Wq"][:, cols.reshape(-1)], a["L0_ffn_Wk"][:, cols.reshape(-1)], a["L0_ffn_Wv"], a["L0_ffn_Wo"],
        a["L0_ffn_gate_W"], a["L0_ffn_bq"][cols].T, a["L0_ffn_bk"][cols].T], axis=1)
    arrays["rows_w"] = np.ascontiguousarray(np.broadcast_to(np.concatenate([
        a["L0_ffn_bv"], a["L0_ffn_bo"], a["L0_ffn_ln1_g"], a["L0_ffn_ln1_b"], a["L0_ffn_gate_b"],
        a["L0_ffn_b2"].reshape(-1)]), (R, Q_END)))
    arrays["moe_w"] = np.concatenate([
        a["L0_ffn_W1"].transpose(1, 0, 2).reshape(D, -1),
        a["L0_ffn_W2"].reshape(NE, NC, 128, D).transpose(2, 0, 1, 3).reshape(128, -1),
        a["L0_ffn_b1"].reshape(NE * NC, 128).T], axis=1)

    p = np.arange(128)
    consts = np.zeros((128, C_END), f32)
    consts[:, C_ID:C_ID + 128] = np.eye(128)
    for t in range(NT):
        consts[p % 32 == t, C_BLK + t * R:C_BLK + (t + 1) * R] = -1.0
    consts[:, C_MHI] = p % 32 < 16
    consts[:, C_MLO] = p % 32 >= 16
    consts[:, C_ONE4] = p % 32 < NT
    consts[:, C_REV:C_END] = np.tile(NE - np.arange(NE), NT)
    arrays["consts"] = consts

    nc = _bacc.Bacc("TRN2", target_bir_lowering=False, num_devices=1)
    arrays = {f"in_{k}": np.ascontiguousarray(v) for k, v in arrays.items()}
    args = [nc.dram_tensor(f"in_{k}", arrays[f"in_{k}"].shape, F32, kind="ExternalInput").ap() for k in _IN]
    o = nc.dram_tensor("out", (B, S, D), F32, kind="ExternalOutput").ap()
    tower(nc, *args, o)
    r = _run(nc, [arrays], core_ids=[0])
    return r.results[0]["out"]
```

```python
from contextlib import ExitStack

import concourse.bass as bass
import numpy as np
from concourse import mybir

ALU = mybir.AluOpType
ACT = mybir.ActivationFunctionType
AX = mybir.AxisListType
F32 = mybir.dt.float32
F32R = mybir.dt.float32r
I32 = mybir.dt.int32

B, T, FIN, D, TAPS = 16, 500, 80, 128, 5
S = T - TAPS + 1
NT = 4
R = S // NT
H1, E1 = 8, 64
H2, E2 = 8, 16
G2 = H2 // 4
NE, FF = 8, 512
NC = FF // 128
SEG = H1 * S // 128
EPS = 1e-5
RSQRT_SEED = float(0x5F3759DF)
PADW = 640

C_ID, C_BLK, C_MHI, C_MLO, C_ONE4, C_NLO, C_REV = 0, 128, 624, 625, 626, 627, 632
C_END = C_REV + NT * NE

A_WQ, A_WK, A_WV, A_WLT = 0, 1024, 2048, 3072
A_END = 4096
P_WQ, P_WK, P_WV, P_WO, P_GW = 0, 256, 512, 640, 768
P_BQ, P_BK = 776, 778
P_END = 780
Q_BV, Q_BO, Q_G, Q_BETA, Q_GB, Q_B2 = 0, 128, 256, 384, 512, 520
Q_END = Q_B2 + NE * D
N_W, N_B, N_GAMMA, N_BETA = 0, TAPS * D, TAPS * D + 1, TAPS * D + 2
N_END = TAPS * D + 3
M_W1, M_W2, M_B1 = 0, NE * FF, 2 * NE * FF
M_END = 2 * NE * FF + NE * NC


def offset(h):
    return (h * S) % 128


def pieces(h):
    first = h * S // 128
    n = (offset(h) + S + 127) // 128
    return [(first + c, 128 * c, c > 0 or offset(h) == 0, c < n - 1 or (h + 1) * S % 128 == 0)
            for c in range(n)]


class Steps:

    def __init__(self, eng, sem):
        self.eng, self.sem, self.before, self.n = eng, sem, 0, 0

    def loop(self, i, per):
        self.outer, self.per = self.n, per
        self.before, self.n = i * per + self.outer, 0

    def end(self, trips):
        assert self.n == self.per, (self.n, self.per)
        self.before, self.n = 0, self.outer + trips * self.per

    def did(self, ins):
        ins.then_inc(self.sem, 1)
        self.n += 1

    def wait(self):
        self.eng.wait_ge(self.sem, self.before + self.n)


def tower(nc, xt, conv_w, att1_w, att2_w, rows_w, moe_w, consts, out):
    with ExitStack() as whole:
        def sem(name):
            return whole.enter_context(nc.semaphore(name))

        def sb(name, shape, dt=F32, ctx=whole):
            return ctx.enter_context(nc.sbuf_tensor(name, shape, dt))

        feat = sb("feat", [128, (B + 2) * S])
        toks = sb("toks", [128, B * NT * D])
        xin = toks[0:FIN, 0:B * T]
        resid = toks[0:R, :].rearrange("p (b n) -> p b n", b=B)
        cst = sb("cst", [128, C_END])
        ident = cst[:, C_ID:C_ID + 128]
        mask_hi, mask_lo = cst[:, C_MHI:C_MHI + 1], cst[:, C_MLO:C_MLO + 1]
        ones4 = cst[:, C_ONE4:C_ONE4 + 1]
        moe = sb("moe", [128, M_END])
        gates = sb("gates", [R, (B + 1) * NT * NE])
        gates_b = gates[:, :].rearrange("p (b n) -> p b n", b=B + 1)
        rows = sb("rows", [R, Q_END])
        bn_st = sb("bn_st", [128, B, 6])
        bn_mv = sb("bn_mv", [128, 2])
        bn_s = sb("bn_s", [128, 4])
        ln_st = sb("ln_st", [R, NT, 6])
        ln_mv = sb("ln_mv", [R, NT, 2])
        ln_v = sb("ln_v", [128, NT])
        ln_r = sb("ln_r", [128, NT])
        ln_t = sb("ln_t", [128, NT])
        ln_out = sb("ln_out", [R, NT, D])
        mx = sb("mx", [R, NT])

        early = ExitStack()
        cw = sb("cw", [128, N_END], ctx=early)
        h1f = sb("h1f", [128, S], ctx=early)
        early.close()

        a1 = ExitStack()
        w_hi = sb("w_hi", [128, A_WLT], F32R, ctx=a1)
        w_lo = sb("w_lo", [128, A_WLT], F32R, ctx=a1)
        wlt = sb("wlt", [128, H1, D], ctx=a1)
        z_hi = sb("z_hi", [128, S], F32R, ctx=a1)
        z_lo = sb("z_lo", [128, S], F32R, ctx=a1)
        xa = sb("xa", [128, S], F32R, ctx=a1)
        xb = sb("xb", [128, S], F32R, ctx=a1)
        ya = sb("ya", [128, S], F32R, ctx=a1)
        yb = sb("yb", [128, S], F32R, ctx=a1)
        val = sb("val", [R, NT, H1, D + 1], ctx=a1)
        prob = [sb(f"prob{i}", [R, NT, PADW], ctx=a1) for i in range(2)]
        mixed = sb("mixed", [128, D * SEG], ctx=a1)
        raw = mixed[:, 0:A_WLT]
        rden = sb("rden", [128, (SEG + 2) // 3, 3], ctx=a1)
        a1.close()

        a2 = ExitStack()
        w2a = sb("w2a", [128, P_END], ctx=a2)
        v_hi = sb("v_hi", [128, P_WV], F32R, ctx=a2)
        v_lo = sb("v_lo", [128, P_WV], F32R, ctx=a2)
        zc = sb("zc", [128, S], ctx=a2)
        zc_hi = sb("zc_hi", [128, S], F32R, ctx=a2)
        zc_lo = sb("zc_lo", [128, S], F32R, ctx=a2)
        zres = sb("zres", [128, S], ctx=a2)
        q_hi = sb("q_hi", [128, S], F32R, ctx=a2)
        q_part = sb("q_part", [128, S], ctx=a2)
        k_part = sb("k_part", [128, S], ctx=a2)
        q_mix = sb("q_mix", [128, S], F32R, ctx=a2)
        side = sb("side", [128, 1 + 2 * G2], ctx=a2)
        ka = [sb(f"ka{i}", [128, S], F32R, ctx=a2) for i in range(2)]
        kb = [sb(f"kb{i}", [128, S], F32R, ctx=a2) for i in range(2)]
        qa = [sb(f"qa{i}", [128, S], F32R, ctx=a2) for i in range(4)]
        qb = [sb(f"qb{i}", [128, S], F32R, ctx=a2) for i in range(4)]
        val2 = sb("val2", [R, NT, H2, 32], ctx=a2)
        prob2 = [sb(f"prob2_{i}", [R, NT, S], ctx=a2) for i in range(4)]
        o4 = sb("o4", [128, S], ctx=a2)
        rden2 = sb("rden2", [R, NT * 4], ctx=a2)
        o_tok = sb("o_tok", [R, NT, D], ctx=a2)
        o_feat = sb("o_feat", [128, S], ctx=a2)
        u = sb("u", [R, NT, D], ctx=a2)
        tc = sb("tc", [128, S], ctx=a2)
        lg = sb("lg", [R, NT, NE], ctx=a2)
        lmax = sb("lmax", [R, NT], ctx=a2)
        lexp = sb("lexp", [R, NT, NE], ctx=a2)
        lden = sb("lden", [R, NT], ctx=a2)
        pick = sb("pick", [R, NT, NE], ctx=a2)
        a2.close()

        a3 = ExitStack()
        hid = [sb(f"hid{i}", [128, NC, S], ctx=a3) for i in range(2)]
        acc = [sb(f"acc{i}", [R, NT, D], ctx=a3) for i in range(2)]
        term = [sb(f"term{i}", [R, NT, D], ctx=a3) for i in range(2)]
        gb_now = sb("gb_now", [R, NT, NE], ctx=a3)
        a3.close()

        ps = whole.enter_context(nc.psum_tensor("ps", [128, 8, 512], F32))
        sc = ps[:, 0:4, :]
        px, py, po = ps[:, 4, :], ps[:, 5, :], [ps[:, 6, :], ps[:, 7, :]]
        pair = [ps[:, 2 * i:2 * i + 2, :] for i in range(3)]
        pv, pm = ps[:, 6, :], ps[:, 7, :]

        def tiles(bank, w=D):
            return bank[0:R, 0:NT * w].rearrange("p (t n) -> p t n", t=NT)

        d_x = [sem(f"d_x{i}") for i in range(4)]
        d_cw, d_cst, d_a1, d_a2, d_rows, d_moe = (sem(n) for n in ("d_cw", "d_cst", "d_a1", "d_a2", "d_rows", "d_moe"))
        d_out = [sem("d_out0"), sem("d_out1")]
        dve_step = sem("dve_step")
        held = sem("held")
        pool_step = sem("pool_step")
        conv_done, relu_done, stats_done, bn_ready = (sem(n) for n in ("conv_done", "relu_done", "stats_done", "bn_ready"))
        bn_applied, h1_turned, h1_kept, z1_ready, z1_turned, z1_kept = (sem(n) for n in (
            "bn_applied", "h1_turned", "h1_kept", "z1_ready", "z1_turned", "z1_kept"))
        w1_split, ones_set = sem("w1_split"), sem("ones_set")
        z_split, x_made, y_made, x_hi, y_hi, x_lo, y_lo = (sem(n) for n in (
            "z_split", "x_made", "y_made", "x_hi", "y_hi", "x_lo", "y_lo"))
        v_made, v_kept, s_made, max_done, max_turned, max_kept, st_made, exp_done = (sem(n) for n in (
            "v_made", "v_kept", "s_made", "max_done", "max_turned", "max_kept", "st_made", "exp_done"))
        pads_zero, seg_made, seg_kept, head_mixed, lt_made, h2_kept, z2_ready, z2_turned, z2_kept = (sem(n) for n in (
            "pads_zero", "seg_made", "seg_kept", "head_mixed", "lt_made", "h2_kept", "z2_ready", "z2_turned", "z2_kept"))
        w2_split, z2_split, zc_ready, zres_ready, zeroed = (sem(n) for n in (
            "w2_split", "z2_split", "zc_ready", "zres_ready", "zeroed"))
        q_made, k_made, v2_made, q_hi_done, q_part_done, k_part_done, q_mixed, k_mixed, v2_kept, qa_done, qb_done = (
            sem(n) for n in ("q_made", "k_made", "v2_made", "q_hi_done", "q_part_done", "k_part_done", "q_mixed",
                             "k_mixed", "v2_kept", "qa_done", "qb_done"))
        ka_done = sem("ka_done")
        s2_made, max2_done, max2_turned, max2_kept, st2_made, exp2_done = (sem(n) for n in (
            "s2_made", "max2_done", "max2_turned", "max2_kept", "st2_made", "exp2_done"))
        o4_made, o4_kept, o4_turned, o_tok_done, of_turned, of_kept, wo_made, u_done = (sem(n) for n in (
            "o4_made", "o4_kept", "o4_turned", "o_tok_done", "of_turned", "of_kept", "wo_made", "u_done"))
        ln3_done, t_ready, t_turned, t_kept, lg_made, lg_done, lsub_done, lexp_done, gates_kept = (sem(n) for n in (
            "ln3_done", "t_ready", "t_turned", "t_kept", "lg_made", "lg_done", "lsub_done", "lexp_done", "gates_kept"))
        hid_made, gelu_done, y_moe_made, y_moe_used, acc_done = (sem(n) for n in (
            "hid_made", "gelu_done", "y_moe_made", "y_moe_used", "acc_done"))

        USES = 4 * H2
        PAIR = [(u + 2) % 3 if u < USES - 2 else u % 3 for u in range(USES)]
        FIRST_USE = USES - 4

        def pair_free(pe, n, use):
            if use >= FIRST_USE and isinstance(n, int):
                return
            before = max(v for v in range(use - USES, use) if PAIR[v % USES] == PAIR[use])
            k, kind = before // 4, before % 4
            slot = use // 4
            head = n - (slot + (use % 4 < 2)) + k
            if kind < 2:
                pe.wait_ge(max2_done, 2 * (head + 1) + kind + 1)
            else:
                pe.wait_ge(exp2_done, 2 + 2 * head + kind - 1)

        def hold(eng):
            eng.sem_inc(held, 1)

        def feat_b(b):
            return feat[:, bass.ds((b + 1) * S, S)]

        NSEG_GROUPS = (SEG + 2) // 3
        A_PART, B_PART = 3, 4
        xw = w_hi[:, :].rearrange("p (w h n) -> p w h n", w=3, h=H1)
        xwl = w_lo[:, :].rearrange("p (w h n) -> p w h n", w=3, h=H1)

        def groups_in(h, a, b):
            return [w // 3 for w, _, _, last in pieces(h)[a:b] if last and (w % 3 == 2 or w == SEG - 1)]

        out_v = out.rearrange("b (t p) d -> p (b t) d", p=R)

        block = whole.enter_context(nc.Block())

        @block.sync
        def _(sp):
            for s in d_out:
                sp.sem_inc(s, 1)
            sp.dma_start(cw[:, :], conv_w).then_inc(d_cw, 16)
            for i in range(4):
                n = B * T // 4
                sp.dma_start(xin[:, i * n:(i + 1) * n], xt[:, i * n:(i + 1) * n]).then_inc(d_x[i], 16)
            sp.dma_start(cst[:, :], consts).then_inc(d_cst, 16)
            sp.dma_start(rows[:, :], rows_w).then_inc(d_rows, 16)
            sp.dma_start(moe[:, :], moe_w).then_inc(d_moe, 16)
            sp.wait_ge(z1_kept, 1 + B)
            sp.dma_start(raw, att1_w[:, 0:A_WLT]).then_inc(d_a1, 16)
            sp.dma_start(wlt[:, :, :].rearrange("p c n -> p (c n)"), att1_w[:, A_WLT:A_END]).then_inc(d_a1, 16)
            sp.wait_ge(z2_kept, 1 + B)
            sp.dma_start(w2a[:, :], att2_w).then_inc(d_a2, 16)
            with sp.Fori(0, B // 2) as i:
                for k in range(2):
                    sp.wait_ge(acc_done, i * 2 + k + 1)
                    sp.dma_start(out_v[:, bass.ds((i * 2 + k) * NT, NT), :], acc[k][:, :, :]).then_inc(d_out[k], 16)
            sp.wait_ge(d_out[0], 1 + 16 * B // 2)
            sp.wait_ge(d_out[1], 1 + 16 * B // 2)

        @block.tensor
        def _(pe):
            for s in (h1_turned, z1_turned, lt_made):
                pe.sem_inc(s, 1)
            pe.sem_inc(st2_made, 8)
            pe.wait_ge(d_cw, 16)
            for i in range(4):
                pe.wait_ge(d_x[i], 16)
            with pe.Fori(0, B // 2) as i:
                for k in range(2):
                    pe.wait_ge(relu_done, 1 + i * 2)
                    bank = (px, py)[k]
                    for tap in range(TAPS):
                        mm = pe.matmul(bank[:, 0:S], cw[0:FIN, N_W + tap * D:N_W + (tap + 1) * D],
                                       xin[:, bass.ds((i * 2 + k) * T + tap, S)],
                                       start=tap == 0, stop=tap == TAPS - 1)
                    mm.then_inc(conv_done, 1)
            pe.wait_ge(d_cst, 16)
            with pe.Fori(0, B) as b:
                pe.wait_ge(bn_applied, b + 1)
                pe.wait_ge(h1_kept, 1 + b)
                for t in range(NT):
                    mm = pe.transpose(tiles(px)[:, t, :], h1f[:, t * R:(t + 1) * R], ident)
                mm.then_inc(h1_turned, 1)
                pe.wait_ge(z1_ready, b + 1)
                pe.wait_ge(z1_kept, 1 + b)
                for t in range(NT):
                    mm = pe.transpose(py[:, t * R:(t + 1) * R], ln_out[:, t, :], ident[0:R, 0:R])
                mm.then_inc(z1_turned, 1)
            pe.wait_ge(w1_split, 2)
            pe.wait_ge(ones_set, 1)

            def split_product(dst, lhs_hi, lhs_lo, rhs_hi, rhs_lo):
                pe.matmul(dst, lhs_hi, rhs_lo, start=True, stop=False)
                pe.matmul(dst, lhs_lo, rhs_hi, start=False, stop=False)
                return pe.matmul(dst, lhs_hi, rhs_hi, start=False, stop=True)

            def project(h):
                split_product(px[:, 0:S], xw[:, 0, h, :], xwl[:, 0, h, :], z_hi[:, :], z_lo[:, :]).then_inc(x_made, 1)
                split_product(py[:, 0:S], xw[:, 1, h, :], xwl[:, 1, h, :], z_hi[:, :], z_lo[:, :]).then_inc(y_made, 1)

            def values(b, i):
                t, half = i % NT, i // NT
                if i >= 2:
                    pe.wait_ge(v_kept, b * 8 + i - 1)
                w = slice(A_WV + 512 * half, A_WV + 512 * (half + 1))
                tok = slice(t * R, (t + 1) * R)
                split_product(po[i % 2][0:R, :], z_hi[:, tok], z_lo[:, tok], w_hi[:, w], w_lo[:, w]).then_inc(v_made, 1)

            def maxima(b, h):
                pe.wait_ge(x_hi, b * H1 + h + 1)
                pe.wait_ge(x_lo, b * H1 + h + 1)
                pe.wait_ge(y_hi, b * H1 + h + 1)
                pe.wait_ge(exp_done, 1 + b * H1 + h)
                for t in range(NT):
                    mm = pe.matmul(sc[0:R, t, 0:S], xa[:, t * R:(t + 1) * R], ya[:, :], start=True, stop=True)
                mm.then_inc(s_made, 1)

            def turn_max(b, h):
                pe.wait_ge(max_done, b * H1 + h + 1)
                pe.matmul(px[64:64 + NT, 0:R], mx[:, :], ident[0:R, 0:R], start=True, stop=True).then_inc(max_turned, 1)

            def scores(b, h):
                pe.wait_ge(max_kept, b * H1 + h + 1)
                pe.wait_ge(y_lo, b * H1 + h + 1)
                for t in range(NT):
                    tok = slice(t * R, (t + 1) * R)
                    pe.matmul(sc[0:R, t, 0:S], yb[0:E1 + NT, tok], xb[0:E1 + NT, :], start=True, stop=False)
                    mm = pe.matmul(sc[0:R, t, 0:S], ya[:, tok], xa[:, :], start=False, stop=True)
                mm.then_inc(st_made, 1)

            def mix(b, h, first, last):
                todo = pieces(h)
                for w, col, opens, closes in todo[first:last]:
                    bank, at = po[w // 3 % 2], w % 3 * (D + 1)
                    if opens and w % 3 == 0 and w >= 6:
                        pe.wait_ge(seg_kept, b * NSEG_GROUPS + w // 3 - 1)
                    for t in range(NT):
                        mm = pe.matmul(bank[:, at:at + D + 1], prob[h % 2][:, t, col:col + 128], val[:, t, h, :],
                                       start=opens and t == 0, stop=closes and t == NT - 1)
                    if closes and (w % 3 == 2 or w == SEG - 1):
                        mm.then_inc(seg_made, 1)

            with pe.Fori(0, B) as b:
                pe.wait_ge(z_split, b + 1)
                pe.wait_ge(h2_kept, 1 + b)
                pe.wait_ge(z2_kept, 1 + b)
                project(0)
                for i in range(4):
                    values(b, i)
                maxima(b, 0)
                for i in range(4, 8):
                    values(b, i)
                turn_max(b, 0)
                scores(b, 0)
                project(1)
                for h in range(1, H1):
                    maxima(b, h)
                    pe.wait_ge(pads_zero, b * H1 + h)
                    pe.wait_ge(v_kept, b * 8 + 8)
                    mix(b, h - 1, 0, A_PART)
                    turn_max(b, h)
                    mix(b, h - 1, A_PART, B_PART)
                    scores(b, h)
                    if h < H1 - 1:
                        project(h + 1)
                    mix(b, h - 1, B_PART, 9)
                pe.wait_ge(exp_done, 1 + (b + 1) * H1)
                pe.wait_ge(pads_zero, (b + 1) * H1)
                mix(b, H1 - 1, 0, 9)
                pe.wait_ge(seg_kept, (b + 1) * NSEG_GROUPS)
                for t in range(NT):
                    for c in range(H1):
                        a = H1 * R * t + c
                        mm = pe.matmul(tiles(px)[:, t, :], mixed[:, a:a + H1 * (R - 1) + 1:H1], wlt[:, c, :],
                                       start=c == 0, stop=c == H1 - 1)
                mm.then_inc(lt_made, 1)
                pe.wait_ge(z2_ready, b + 1)
                for t in range(NT):
                    mm = pe.transpose(py[:, t * R:(t + 1) * R], ln_out[:, t, :], ident[0:R, 0:R])
                mm.then_inc(z2_turned, 1)

            pe.wait_ge(w2_split, 2)
            pe.wait_ge(zeroed, 1)

            def values2(m, g):
                for t in range(NT):
                    mm = pe.matmul(tiles(pv, 64)[:, t, :], zc[:, t * R:(t + 1) * R],
                                   w2a[:, P_WV + 64 * g:P_WV + 64 * (g + 1)], start=True, stop=True)
                mm.then_inc(v2_made, 1)

            def project2(base, g, made):
                w = slice(base + 128 * g, base + 128 * (g + 1))
                split_product(pm[:, 0:S], v_hi[:, w], v_lo[:, w], zc_hi[:, :], zc_lo[:, :]).then_inc(made, 1)

            def maxima2(n, g, j, use):
                pe.wait_ge(qa_done, 1 + n + 1)
                for half in range(2):
                    pair_free(pe, n, use + half)
                    for t in range(2):
                        tok = slice((2 * half + t) * R, (2 * half + t + 1) * R)
                        mm = pe.matmul(pair[PAIR[use + half]][0:R, t, 0:S], qa[j][:, tok], ka[g][:, :], start=True, stop=True)
                    mm.then_inc(s2_made, 1)

            def turn_max2(n, j):
                pe.wait_ge(max2_done, 2 * n + 2)
                pe.matmul(pm[32 * j:32 * j + NT, 0:R], mx[:, :], ident[0:R, 0:R], start=True, stop=True,
                          tile_position=(0, 32 * j)).then_inc(max2_turned, 1)

            def scores2(n, g, j, use):
                pe.wait_ge(max2_kept, n + 1)
                for half in range(2):
                    pair_free(pe, n, use + half)
                    for t in range(2):
                        tok = slice((2 * half + t) * R, (2 * half + t + 1) * R)
                        dst = pair[PAIR[use + half]][0:R, t, 0:S]
                        pe.matmul(dst, kb[g][:, tok], qb[j][:, :], start=True, stop=False)
                        mm = pe.matmul(dst, ka[g][:, tok], qa[j][:, :], start=False, stop=True)
                    mm.then_inc(st2_made, 1)

            def mix2(m, g):
                pe.wait_ge(exp2_done, 2 + m * 8)
                pe.wait_ge(v2_kept, 1 + m)
                for t in range(NT):
                    for j in range(4):
                        mm = pe.matmul(pv[32 * j:32 * j + 32, 0:S], val2[:, t, 4 * g + j, :], prob2[j][:, t, :],
                                       start=t == 0, stop=t == NT - 1, tile_position=(0, 32 * j))
                mm.then_inc(o4_made, 1)

            def turn_o4(m):
                pe.wait_ge(o4_kept, m + 1)
                for t in range(NT):
                    mm = pe.transpose(tiles(pv)[:, t, :], o4[:, t * R:(t + 1) * R], ident)
                mm.then_inc(o4_turned, 1)

            def turn_o(m):
                pe.wait_ge(o_tok_done, m + 1)
                for t in range(NT):
                    mm = pe.transpose(pv[:, t * R:(t + 1) * R], o_tok[:, t, :], ident[0:R, 0:R])
                mm.then_inc(of_turned, 1)

            def out_product(b):
                pe.wait_ge(of_kept, b + 1)
                pe.wait_ge(zres_ready, 1 + b)
                for t in range(NT):
                    tok = slice(t * R, (t + 1) * R)
                    pe.matmul(tiles(pv)[:, t, :], zres[:, tok], ident, start=True, stop=False)
                    mm = pe.matmul(tiles(pv)[:, t, :], o_feat[:, tok], w2a[:, P_WO:P_WO + D], start=False, stop=True)
                mm.then_inc(wo_made, 1)

            def turn_t(b):
                pe.wait_ge(t_ready, b + 1)
                for t in range(NT):
                    mm = pe.transpose(pv[:, t * R:(t + 1) * R], ln_out[:, t, :], ident[0:R, 0:R])
                mm.then_inc(t_turned, 1)

            def logits(b):
                pe.wait_ge(t_kept, b + 1)
                for t in range(NT):
                    mm = pe.matmul(tiles(pv, NE)[:, t, :], tc[:, t * R:(t + 1) * R], w2a[:, P_GW:P_GW + NE],
                                   start=True, stop=True)
                mm.then_inc(lg_made, 1)

            pe.wait_ge(z2_split, 1)
            pe.wait_ge(zc_ready, 1)
            values2(0, 0)
            project2(P_WQ, 0, q_made)
            pe.wait_ge(q_mixed, 1)
            project2(P_WK, 0, k_made)
            pe.wait_ge(k_mixed, 1)
            pe.wait_ge(v2_kept, 2)
            maxima2(0, 0, 0, FIRST_USE)
            with pe.Fori(0, B) as b:
                for g in range(G2):
                    m, other = b * G2 + g, 1 - g
                    for j in range(4):
                        n, use = b * H2 + 4 * g + j, 4 * (4 * g + j)
                        if j == 2:
                            pe.wait_ge(q_mixed, m + 2)
                        if j == 3:
                            pe.wait_ge(k_mixed, m + 2)
                        turn_max2(n, j)
                        maxima2(n + 1, g if j < 3 else other, (j + 1) % 4, use)
                        if j == 0:
                            if g == 0:
                                pe.wait_ge(lg_done, 1 + b)
                            else:
                                pe.wait_ge(u_done, b + 1)
                            mix2(m, other)
                        if j == 1:
                            pe.wait_ge(o_tok_done, m + 1)
                            if g == 1:
                                pe.wait_ge(zc_ready, b + 2)
                                pe.wait_ge(z2_split, b + 2)
                            values2(m + 1, other)
                            pe.wait_ge(max2_kept, n + 1)
                            project2(P_WQ, other, q_made)
                        if j == 2:
                            pe.wait_ge(max2_kept, n + 1)
                            project2(P_WK, other, k_made)
                        scores2(n, g, j, use + 2)
                        if j == 0:
                            turn_o4(m)
                        if j == 1:
                            pe.wait_ge(v2_kept, m + 3)
                            if g == 0:
                                turn_o(m)
                            else:
                                turn_t(b)
                        if j == 2:
                            if g == 0:
                                out_product(b)
                            else:
                                logits(b)
            pe.wait_ge(lg_done, 1 + B)
            mix2(B * G2, 1)
            turn_o4(B * G2)
            turn_o(B * G2)
            out_product(B)
            pe.wait_ge(u_done, B + 1)
            turn_t(B)
            logits(B)

            pe.wait_ge(d_moe, 16)
            pe.wait_ge(gates_kept, B + 1)
            w1 = moe[:, M_W1:M_W2].rearrange("p (e n) -> p e n", e=NE)
            w2 = moe[:, M_W2:M_B1].rearrange("p (e c n) -> p e c n", e=NE, c=NC)

            def up(b, e):
                for c in range(NC):
                    pe.wait_ge(gelu_done, 1 + ((b * NE + e) * NC + c - (NC - 1) if e else b * NE * NC))
                    pe.matmul(sc[:, c, 0:S], w1[:, e, c * 128:(c + 1) * 128], feat_b(b), start=True, stop=True).then_inc(hid_made, 1)

            def down(b, e):
                pe.wait_ge(gelu_done, 1 + (b * NE + e + 1) * NC)
                if e >= 2:
                    pe.wait_ge(y_moe_used, 1 + b * NE + e - 1)
                else:
                    pe.wait_ge(y_moe_used, 1 + b * NE)
                for t in range(NT):
                    for c in range(NC):
                        mm = pe.matmul(tiles(po[e % 2])[:, t, :], hid[e % 2][:, c, t * R:(t + 1) * R], w2[:, e, c, :],
                                       start=c == 0, stop=c == NC - 1)
                mm.then_inc(y_moe_made, 1)

            with pe.Fori(0, B) as b:
                up(b, 0)
                for e in range(1, NE):
                    up(b, e)
                    down(b, e - 1)
                down(b, NE - 1)

        @block.scalar
        def _(act):
            for s in (relu_done, h1_kept, z1_kept, exp_done, z2_kept, qa_done, gelu_done):
                act.sem_inc(s, 1)
            act.sem_inc(exp2_done, 2)
            act.wait_ge(d_cw, 16)
            act.wait_ge(d_cst, 16)
            with act.Fori(0, B // 2) as i:
                for k, bank in enumerate((px, py)):
                    act.wait_ge(conv_done, i * 2 + k + 1)
                    act.activation(feat_b(i * 2 + k), bank[:, 0:S], ACT.Relu, bias=cw[:, N_B:N_B + 1]).then_inc(relu_done, 1)
            act.wait_ge(bn_ready, 1)
            with act.Fori(0, B) as b:
                act.wait_ge(h1_turned, 1 + b)
                act.activation(h1f[:, :], feat_b(b), ACT.Identity, bias=bn_s[:, 3:4], scale=bn_s[:, 2:3]).then_inc(bn_applied, 1)
                act.wait_ge(h1_turned, 1 + b + 1)
                hold(act)
                act.copy(resid[:, bass.ds(b, 1), :].rearrange("p a n -> p (a n)"), px[0:R, :]).then_inc(h1_kept, 1)
                act.wait_ge(z1_turned, 1 + b + 1)
                hold(act)
                act.copy(feat_b(b), py[:, 0:S]).then_inc(z1_kept, 1)

            def high_parts(b, h):
                act.wait_ge(x_made, b * H1 + h + 1)
                act.copy(xb[:, :], px[:, 0:S])
                act.copy(xa[0:E1, :], px[0:E1, 0:S]).then_inc(x_hi, 1)
                act.wait_ge(y_made, b * H1 + h + 1)
                act.copy(ya[:, :], py[:, 0:S]).then_inc(y_hi, 1)

            with act.Fori(0, B) as b:
                high_parts(b, 0)
                for i in range(8):
                    act.wait_ge(v_made, b * 8 + i + 1)
                    t, half = i % NT, i // NT
                    act.copy(val[:, t, 4 * half:4 * half + 4, 0:D],
                             po[i % 2][0:R, :].rearrange("p (h n) -> p h n", h=4)).then_inc(v_kept, 1)
                for h in range(H1):
                    act.wait_ge(st_made, b * H1 + h + 1)
                    act.activation(prob[h % 2][:, :, offset(h):offset(h) + S], sc[0:R, :, 0:S], ACT.Exp,
                                   scale=1.0 / E1).then_inc(exp_done, 1)
                    if h < H1 - 1:
                        high_parts(b, h + 1)
                act.wait_ge(z2_turned, b + 1)
                hold(act)
                act.copy(feat_b(b), py[:, 0:S]).then_inc(z2_kept, 1)

            act.wait_ge(d_a2, 16)
            act.wait_ge(zeroed, 1)
            act.wait_ge(w2_split, 2)

            def q_high(m, g):
                act.wait_ge(q_made, m + 1)
                act.wait_ge(qb_done, 4 + m * 4)
                act.activation(q_hi[:, :], pm[:, 0:S], ACT.Identity, bias=w2a[:, P_BQ + g:P_BQ + g + 1]).then_inc(q_hi_done, 1)
                act.wait_ge(q_hi_done, m + 1)
                act.activation(q_part[:, :], q_hi[:, :].bitcast(F32), ACT.Identity, bias=side[:, 1 + g:2 + g],
                               scale=side[:, 0:1]).then_inc(q_part_done, 1)

            def k_high(m, g):
                act.wait_ge(k_made, m + 1)
                act.activation(ka[g][:, :], pm[:, 0:S], ACT.Identity, bias=w2a[:, P_BK + g:P_BK + g + 1]).then_inc(ka_done, 1)
                act.wait_ge(ka_done, m + 1)
                act.activation(k_part[:, :], ka[g][:, :].bitcast(F32), ACT.Identity, bias=side[:, 3 + g:4 + g],
                               scale=cst[:, C_NLO:C_NLO + 1]).then_inc(k_part_done, 1)

            def keep_qa(m, j):
                rows_j = slice(32 * j, 32 * j + 32)
                act.wait_ge(q_mixed, m + 1)
                act.wait_ge(st2_made, m * 8 + 2 * j + 2)
                act.copy(qa[j][rows_j, :], q_mix[rows_j, :].bitcast(F32)).then_inc(qa_done, 1)

            def exps(n, j, use):
                for half in range(2):
                    act.wait_ge(st2_made, 8 + 2 * n + half + 1)
                    act.activation(prob2[j][:, 2 * half:2 * half + 2, :], pair[PAIR[use + half]][0:R, :, 0:S], ACT.Exp,
                                   scale=float(E2) ** -0.5).then_inc(exp2_done, 1)

            def keep_o4(m):
                act.wait_ge(o4_made, m + 1)
                act.copy(o4[:, :], pv[:, 0:S]).then_inc(o4_kept, 1)

            def keep_of(b):
                act.wait_ge(of_turned, b + 1)
                act.copy(o_feat[:, :], pv[:, 0:S]).then_inc(of_kept, 1)

            def keep_t(b):
                act.wait_ge(t_turned, b + 1)
                hold(act)
                act.copy(feat[:, bass.ds(b * S, S)], pv[:, 0:S])
                act.copy(tc[:, :], pv[:, 0:S]).then_inc(t_kept, 1)

            def exp_logits(b):
                act.wait_ge(lsub_done, b + 1)
                act.activation(lexp[:, :, :], lg[:, :, :], ACT.Exp).then_inc(lexp_done, 1)

            q_high(0, 0)
            k_high(0, 0)
            for j in range(3):
                keep_qa(0, j)
            with act.Fori(0, B) as b:
                for g in range(G2):
                    m, n, other = b * G2 + g, b * H2 + 4 * g, 1 - g
                    use = [4 * (4 * g + j) + 2 for j in range(4)]
                    keep_qa(m, 3)
                    keep_o4(m)
                    exps(n, 0, use[0])
                    q_high(m + 1, other)
                    exps(n + 1, 1, use[1])
                    if g == 0:
                        keep_of(b)
                    else:
                        keep_t(b)
                    k_high(m + 1, other)
                    keep_qa(m + 1, 0)
                    exps(n + 2, 2, use[2])
                    keep_qa(m + 1, 1)
                    if g == 1:
                        exp_logits(b)
                    exps(n + 3, 3, use[3])
                    keep_qa(m + 1, 2)
            keep_o4(B * G2)
            keep_of(B)
            keep_t(B)
            exp_logits(B)

            b1 = moe[:, M_B1:M_END]
            act.wait_ge(d_moe, 16)
            with act.Fori(0, B) as b:
                for e in range(NE):
                    if e >= 2:
                        act.wait_ge(y_moe_made, b * NE + e - 1)
                    for c in range(NC):
                        act.wait_ge(hid_made, (b * NE + e) * NC + c + 1)
                        act.activation(hid[e % 2][:, c, :], sc[:, c, 0:S], ACT.Gelu_apprx_tanh,
                                       bias=b1[:, e * NC + c:e * NC + c + 1]).then_inc(gelu_done, 1)

        @block.vector
        def _(dve):
            for s in (h2_kept, v2_kept, lg_done, zres_ready, y_moe_used):
                dve.sem_inc(s, 1)
            step = Steps(dve, dve_step)

            def rsqrt(out_, var, scratch, v):
                step.did(dve.tensor_scalar(v, var, EPS, None, ALU.add))
                step.wait()
                step.did(dve.tensor_scalar(out_.bitcast(I32), v.bitcast(I32), -0.5, RSQRT_SEED, ALU.mult, ALU.add))
                step.wait()
                for _ in range(3):
                    step.did(dve.scalar_tensor_tensor(out=scratch, in0=out_, scalar=-0.5, in1=out_, op0=ALU.mult, op1=ALU.mult))
                    step.wait()
                    step.did(dve.tensor_tensor(scratch, scratch, v, ALU.mult))
                    step.wait()
                    step.did(dve.scalar_tensor_tensor(out=out_, in0=scratch, scalar=1.5, in1=out_, op0=ALU.add, op1=ALU.mult))
                    step.wait()

            def layer_norm(src):
                hold(dve)
                for t in range(NT):
                    st = dve.bn_stats(ln_st[:, t, :], src[:, t, :])
                step.did(st)
                step.wait()
                hold(dve)
                for t in range(NT):
                    st = dve.bn_aggr(ln_mv[:, t, :], ln_st[:, t, :])
                step.did(st)
                step.wait()
                rsqrt(ln_r[0:R, :], ln_mv[:, :, 1], ln_t[0:R, :], ln_v[0:R, :])
                for t in range(NT):
                    last = dve.tensor_scalar(ln_out[:, t, :], src[:, t, :], ln_mv[:, t, 0:1], ln_r[0:R, t:t + 1],
                                             ALU.subtract, ALU.mult)
                return last

            LN_STEPS = 13

            dve.wait_ge(d_cst, 16)
            with dve.Fori(0, B) as b:
                dve.wait_ge(relu_done, 1 + b + 1)
                hold(dve)
                dve.bn_stats(bn_st[:, bass.ds(b, 1), :].rearrange("p a n -> p (a n)"), feat_b(b)).then_inc(stats_done, 1)
            dve.wait_ge(stats_done, B)
            step.did(dve.bn_aggr(bn_mv[:, :], bn_st[:, :, :]))
            step.wait()
            rsqrt(bn_s[:, 0:1], bn_mv[:, 1:2], bn_s[:, 1:2], ln_v[:, 0:1])
            dve.wait_ge(d_cw, 16)
            step.did(dve.tensor_tensor(bn_s[:, 2:3], bn_s[:, 0:1], cw[:, N_GAMMA:N_GAMMA + 1], ALU.mult))
            step.wait()
            step.did(dve.tensor_tensor(bn_s[:, 1:2], bn_s[:, 2:3], bn_mv[:, 0:1], ALU.mult))
            step.wait()
            dve.tensor_tensor(bn_s[:, 3:4], cw[:, N_BETA:N_BETA + 1], bn_s[:, 1:2], ALU.subtract).then_inc(bn_ready, 1)

            with dve.Fori(0, B) as b:
                step.loop(b, LN_STEPS)
                dve.wait_ge(h1_kept, 1 + b + 1)
                dve.wait_ge(z1_turned, 1 + b)
                layer_norm(resid[:, bass.ds(b, 1), :].rearrange("p a (t n) -> p (a t) n", t=NT)).then_inc(z1_ready, 1)
                step.end(B)

            dve.wait_ge(d_a1, 32)
            step.did(dve.tensor_copy(w_hi[:, :], raw))
            step.wait()
            dve.tensor_tensor(w_lo[:, :], raw, w_hi[:, :].bitcast(F32), ALU.subtract).then_inc(w1_split, 2)

            def low_parts(b, h):
                dve.wait_ge(x_hi, b * H1 + h + 1)
                dve.tensor_tensor(xa[E1:128, :], px[E1:128, 0:S], xb[E1:128, :].bitcast(F32), ALU.subtract).then_inc(x_lo, 1)
                dve.wait_ge(y_hi, b * H1 + h + 1)
                dve.tensor_tensor(yb[0:E1, :], py[0:E1, 0:S], ya[0:E1, :].bitcast(F32), ALU.subtract).then_inc(y_lo, 1)

            def keep_group(b, q):
                n = min(3, SEG - 3 * q)
                src = po[q % 2][:, 0:n * (D + 1)].rearrange("p (j n) -> p j n", j=n)
                dve.wait_ge(seg_made, b * NSEG_GROUPS + q + 1)
                step.did(dve.reciprocal(rden[:, q, 0:n], src[:, :, D]))
                step.wait()
                dst = mixed[:, :].rearrange("p (f w) -> p w f", w=SEG)[:, 3 * q:3 * q + n, :]
                dve.tensor_tensor(dst, src[:, :, 0:D], rden[:, q, 0:n].unsqueeze(2).broadcast_to([128, n, D]),
                                  ALU.mult).then_inc(seg_kept, 1)

            def keep_max(rows_, bank, dst, b_h, turned, kept):
                dve.wait_ge(turned, b_h + 1)
                dve.tensor_tensor(dst[rows_, :].rearrange("p (t n) -> p t n", t=NT),
                                  bank[rows_, 0:R].unsqueeze(1).broadcast_to([NT, NT, R]),
                                  cst[rows_, C_BLK:C_BLK + S].rearrange("p (t n) -> p t n", t=NT),
                                  ALU.mult).then_inc(kept, 1)

            with dve.Fori(0, B) as b:
                step.loop(b, 1 + NSEG_GROUPS + LN_STEPS)
                step.did(dve.tensor_copy(z_hi[:, :], feat_b(b)))
                step.wait()
                dve.tensor_tensor(z_lo[:, :], feat_b(b), z_hi[:, :].bitcast(F32), ALU.subtract).then_inc(z_split, 1)
                low_parts(b, 0)
                for h in range(H1):
                    dve.wait_ge(s_made, b * H1 + h + 1)
                    dve.tensor_reduce(mx[:, :], sc[0:R, :, 0:S], AX.X, ALU.max).then_inc(max_done, 1)
                    keep_max(slice(64, 64 + NT), px, xb, b * H1 + h, max_turned, max_kept)
                    if h:
                        for q in groups_in(h - 1, 0, B_PART):
                            keep_group(b, q)
                    if h < H1 - 1:
                        low_parts(b, h + 1)
                    if h:
                        for q in groups_in(h - 1, B_PART, 9):
                            keep_group(b, q)
                for q in groups_in(H1 - 1, 0, 9):
                    keep_group(b, q)
                rb = resid[:, bass.ds(b, 1), :].rearrange("p a n -> p (a n)")
                dve.wait_ge(lt_made, 1 + b + 1)
                dve.tensor_tensor(rb, rb, px[0:R, :], ALU.add).then_inc(h2_kept, 1)
                dve.wait_ge(h2_kept, 1 + b + 1)
                layer_norm(resid[:, bass.ds(b, 1), :].rearrange("p a (t n) -> p (a t) n", t=NT)).then_inc(z2_ready, 1)
                step.end(B)

            dve.wait_ge(d_a2, 16)
            dve.wait_ge(d_rows, 16)
            step.did(dve.tensor_copy(v_hi[:, :], w2a[:, 0:P_WV]))
            step.wait()
            dve.tensor_scalar(side[:, 1:3], w2a[:, P_BQ:P_BQ + 2], mask_lo, None, ALU.mult)
            dve.tensor_scalar(side[:, 3:5], w2a[:, P_BK:P_BK + 2], mask_lo, ones4, ALU.mult, ALU.add)
            dve.tensor_tensor(side[:, 0:1], mask_hi, mask_lo, ALU.subtract)
            dve.tensor_tensor(v_lo[:, :], w2a[:, 0:P_WV], v_hi[:, :].bitcast(F32), ALU.subtract).then_inc(w2_split, 2)
            dve.wait_ge(zeroed, 1)

            def row(c, n=D):
                return rows[:, c:c + n].unsqueeze(1).broadcast_to([R, NT, n])

            def many(a):
                return a.unsqueeze(2).broadcast_to([R, NT, NE])

            def mix_q(m):
                dve.wait_ge(q_part_done, m + 1)
                dve.wait_ge(qa_done, 1 + m * 4)
                dve.scalar_tensor_tensor(out=q_mix[:, :], in0=pm[:, 0:S], scalar=mask_lo, in1=q_part[:, :],
                                         op0=ALU.mult, op1=ALU.add).then_inc(q_mixed, 1)

            def mix_k(m, g):
                dve.wait_ge(k_part_done, m + 1)
                dve.scalar_tensor_tensor(out=kb[g][:, :], in0=pm[:, 0:S], scalar=mask_lo, in1=k_part[:, :],
                                         op0=ALU.mult, op1=ALU.add).then_inc(k_mixed, 1)

            def keep_v2(m, g):
                dve.wait_ge(v2_made, m + 1)
                dve.tensor_tensor(val2[:, :, 4 * g:4 * g + 4, 0:E2],
                                  tiles(pv, 64).rearrange("p t (h n) -> p t h n", h=4),
                                  rows[:, Q_BV + 64 * g:Q_BV + 64 * (g + 1)].rearrange("p (h n) -> p h n", h=4)
                                  .unsqueeze(1).broadcast_to([R, NT, 4, E2]), ALU.add).then_inc(v2_kept, 1)

            def maxima2(n, use):
                for half in range(2):
                    dve.wait_ge(s2_made, 2 * n + half + 1)
                    dve.tensor_reduce(mx[:, 2 * half:2 * half + 2], pair[PAIR[use + half]][0:R, :, 0:S], AX.X,
                                      ALU.max).then_inc(max2_done, 1)

            def norm_o(m, g):
                dve.wait_ge(o4_turned, m + 1)
                o_in = tiles(pv).rearrange("p t (j n) -> p t j n", j=4)
                step.did(dve.reciprocal(rden2[:, :].rearrange("p (t j) -> p t j", t=NT), o_in[:, :, :, E2]))
                step.wait()
                dve.tensor_tensor(o_tok[:, :, 64 * g:64 * (g + 1)].rearrange("p t (j n) -> p t j n", j=4),
                                  o_in[:, :, :, 0:E2],
                                  rden2[:, :].rearrange("p (t j) -> p t j", t=NT).unsqueeze(3).broadcast_to([R, NT, 4, E2]),
                                  ALU.mult).then_inc(o_tok_done, 1)

            def add_bias(b):
                dve.wait_ge(wo_made, b + 1)
                dve.tensor_tensor(u[:, :, :], tiles(pv), row(Q_BO), ALU.add).then_inc(u_done, 1)

            def norm_u(b):
                dve.wait_ge(u_done, b + 1)
                layer_norm(u).then_inc(ln3_done, 1)

            def gate_start(b):
                dve.wait_ge(lg_made, b + 1)
                dve.tensor_tensor(lg[:, :, :], tiles(pv, NE), row(Q_GB, NE), ALU.add).then_inc(lg_done, 1)
                dve.wait_ge(lg_done, 1 + b + 1)
                step.did(dve.tensor_reduce(lmax[:, :], lg[:, :, :], AX.X, ALU.max))
                step.wait()
                dve.tensor_tensor(lg[:, :, :], lg[:, :, :], many(lmax[:, :]), ALU.subtract).then_inc(lsub_done, 1)

            def gate_end(b):
                rev = cst[0:R, C_REV:C_REV + NT * NE].rearrange("p (t n) -> p t n", t=NT)
                dve.wait_ge(lsub_done, b + 1)
                step.did(dve.scalar_tensor_tensor(out=pick[:, :, :], in0=lg[:, :, :], scalar=0.0, in1=rev, op0=ALU.is_equal, op1=ALU.mult))
                step.wait()
                step.did(dve.tensor_reduce(lmax[:, :], pick[:, :, :], AX.X, ALU.max))
                dve.wait_ge(lexp_done, b + 1)
                step.did(dve.tensor_reduce(lden[:, :], lexp[:, :, :], AX.X, ALU.add))
                step.wait()
                dve.tensor_tensor(pick[:, :, :], pick[:, :, :], many(lmax[:, :]), ALU.is_equal)
                step.did(dve.reciprocal(lden[:, :], lden[:, :]))
                step.wait()
                dve.tensor_tensor(gates_b[:, bass.ds(b, 1), :].rearrange("p a (t n) -> p (a t) n", t=NT), pick[:, :, :],
                                  many(lden[:, :]), ALU.mult).then_inc(gates_kept, 1)

            dve.tensor_copy(zc[:, :], feat[:, S:2 * S]).then_inc(zc_ready, 1)
            keep_v2(0, 0)
            mix_q(0)
            mix_k(0, 0)
            maxima2(0, FIRST_USE)
            with dve.Fori(0, B) as b:
                step.loop(b, G2 + LN_STEPS + 1 + 4)
                for g in range(G2):
                    m, other = b * G2 + g, 1 - g
                    for j in range(4):
                        n, use = b * H2 + 4 * g + j, 4 * (4 * g + j)
                        dve.wait_ge(qb_done, 4 + n + 1)
                        keep_max(slice(32 * j, 32 * j + NT), pm, qb[j], n, max2_turned, max2_kept)
                        if j == 1:
                            keep_v2(m + 1, other)
                        if j == 3 and g == 0:
                            add_bias(b)
                        if j == 3 and g == 1:
                            gate_start(b)
                        maxima2(n + 1, use)
                        if j == 0:
                            norm_o(m, other)
                        if j == 1:
                            mix_q(m + 1)
                        if j == 2:
                            mix_k(m + 1, other)
                        if j == 3 and g == 0:
                            dve.tensor_copy(zres[:, :], zc[:, :]).then_inc(zres_ready, 1)
                            dve.wait_ge(zres_ready, 1 + b + 1)
                            dve.tensor_copy(zc[:, :], feat_b(b + 1)).then_inc(zc_ready, 1)
                            norm_u(b)
                        if j == 3 and g == 1:
                            gate_end(b)
                step.end(B)
            norm_o(B * G2, 1)
            add_bias(B)
            norm_u(B)
            gate_start(B)
            gate_end(B)

            dve.wait_ge(gates_kept, B + 1)
            with dve.Fori(0, B // 2) as i:
                step.loop(i, 2 * 2 * NE)
                for k in range(2):
                    b = i * 2 + k
                    step.did(dve.tensor_copy(gb_now[:, :, :], gates_b[:, bass.ds(b + 1, 1), :].rearrange("p a (t n) -> p (a t) n", t=NT)))
                    dve.wait_ge(d_out[k], 1 + i * 16)
                    for e in range(NE):
                        dve.wait_ge(y_moe_made, b * NE + e + 1)
                        dve.tensor_tensor(term[e % 2][:, :, :], tiles(po[e % 2]), row(Q_B2 + e * D), ALU.add).then_inc(y_moe_used, 1)
                        dve.wait_ge(y_moe_used, 1 + b * NE + e + 1)
                        step.wait()
                        step.did(dve.tensor_tensor(term[e % 2][:, :, :], term[e % 2][:, :, :],
                                                   gb_now[:, :, e:e + 1].broadcast_to([R, NT, D]), ALU.mult))
                        step.wait()
                        if e == 0:
                            other = resid[:, bass.ds(b, 1), :].rearrange("p a (t n) -> p (a t) n", t=NT)
                        else:
                            other = acc[k][:, :, :]
                        last = dve.tensor_tensor(acc[k][:, :, :], other, term[e % 2][:, :, :], ALU.add)
                        if e == NE - 1:
                            last.then_inc(acc_done, 1)
                        else:
                            step.did(last)
                step.end(B // 2)

        @block.gpsimd
        def _(pool):
            step = Steps(pool, pool_step)
            pool.sem_inc(qb_done, 4)

            def fill(dst, value):
                step.wait()
                hold(pool)
                step.did(pool.memset(dst, value))

            pool.wait_ge(z1_kept, 1 + B)
            fill(yb[E1:E1 + 32, :].bitcast(F32), 1.0)
            fill(val[:, :, :, D:D + 1], 1.0)
            step.wait()
            pool.sem_inc(ones_set, 1)
            pads = [[(0, offset(h)), (offset(h) + S, (offset(h) + S + 127) // 128 * 128)] for h in range(H1)]
            with pool.Fori(0, B) as b:
                step.loop(b, sum(hi > lo for h in range(H1) for lo, hi in pads[h]))
                for h in range(H1):
                    if h < 2:
                        pool.wait_ge(lt_made, 1 + b)
                    else:
                        pool.wait_ge(max_turned, b * H1 + h + 1)
                    hold(pool)
                    for lo, hi in pads[h]:
                        if hi > lo:
                            fill(prob[h % 2][:, :, lo:hi], 0.0)
                    step.wait()
                    pool.sem_inc(pads_zero, 1)
                step.end(B)
            pool.wait_ge(z2_kept, 1 + B)
            for j in range(4):
                fill(qa[j][:, :].bitcast(F32), 0.0)
                fill(qb[j][:, :].bitcast(F32), 0.0)
                fill(prob2[j][:, :, :], 1.0)
            fill(o_tok[:, :, :], 0.0)
            fill(zres[:, :], 0.0)
            fill(feat[:, (B + 1) * S:(B + 2) * S], 0.0)
            fill(val2[:, :, :, :], 1.0)
            step.wait()
            pool.sem_inc(zeroed, 1)

            def split_z(b):
                hold(pool)
                step.did(pool.tensor_copy(zc_hi[:, :], feat_b(b)))
                step.wait()
                hold(pool)
                pool.tensor_tensor(zc_lo[:, :], feat_b(b), zc_hi[:, :].bitcast(F32), ALU.subtract).then_inc(z2_split, 1)
                pool.wait_ge(z2_split, b + 1)

            def keep_qb(m, j):
                rows_j = slice(32 * j, 32 * j + 32)
                pool.wait_ge(q_hi_done, m + 1)
                pool.wait_ge(st2_made, m * 8 + 2 * j + 2)
                hold(pool)
                pool.tensor_copy(qb[j][rows_j, :], q_hi[rows_j, :].bitcast(F32)).then_inc(qb_done, 1)
                pool.wait_ge(qb_done, 4 + m * 4 + j + 1)

            def scale_t(b):
                pool.wait_ge(ln3_done, b + 1)
                hold(pool)
                wide = [rows[:, c:c + D].unsqueeze(1).broadcast_to([R, NT, D]) for c in (Q_G, Q_BETA)]
                step.did(pool.tensor_tensor(ln_out[:, :, :], ln_out[:, :, :], wide[0], ALU.mult))
                step.wait()
                pool.tensor_tensor(ln_out[:, :, :], ln_out[:, :, :], wide[1], ALU.add).then_inc(t_ready, 1)
                pool.wait_ge(t_ready, b + 1)

            pool.wait_ge(d_rows, 16)
            split_z(0)
            for j in range(3):
                keep_qb(0, j)
            with pool.Fori(0, B) as b:
                step.loop(b, 2)
                for g in range(G2):
                    m = b * G2 + g
                    keep_qb(m, 3)
                    if g == 1:
                        scale_t(b)
                    keep_qb(m + 1, 0)
                    keep_qb(m + 1, 1)
                    if g == 0:
                        pool.wait_ge(k_made, m + 2)
                        split_z(b + 1)
                    keep_qb(m + 1, 2)
                step.end(B)
            scale_t(B)


_IN = ("xt", "conv_w", "att1_w", "att2_w", "rows_w", "moe_w", "consts")


def kernel(**inputs):
    import concourse.bacc as _bacc
    from concourse.bass_utils import run_bass_kernel_spmd as _run

    a = {k: np.asarray(v) for k, v in inputs.items()}
    f32 = np.float32

    def wide(w, n):
        full = np.zeros((128, w.shape[1]), f32)
        full[:n] = w
        return full

    arrays = {}
    arrays["xt"] = np.ascontiguousarray(a["x"].transpose(2, 0, 1).reshape(FIN, B * T))
    w = a["L0_tok_W"].reshape(D, TAPS, FIN).transpose(2, 1, 0).reshape(FIN, TAPS * D)
    arrays["conv_w"] = np.concatenate([wide(w, FIN), a["L0_tok_b"][:, None], a["L0_tok_gamma"][:, None],
                                       a["L0_tok_beta"][:, None]], axis=1)

    def twice(w):
        w = w.transpose(1, 0, 2)
        return np.concatenate([w, w], axis=2).reshape(D, -1)

    arrays["att1_w"] = np.concatenate([
        twice(a["L0_attn_Wk"]), twice(a["L0_attn_Wq"]), a["L0_attn_Wv"].transpose(1, 0, 2).reshape(D, -1),
        a["L0_attn_Wlt"].reshape(H1, 128, D).transpose(1, 0, 2).reshape(128, -1)], axis=1)

    cols = np.array([[16 * (4 * g + p // 32) + p % 16 for p in range(128)] for g in range(G2)])
    arrays["att2_w"] = np.concatenate([
        a["L0_ffn_Wq"][:, cols.reshape(-1)], a["L0_ffn_Wk"][:, cols.reshape(-1)], a["L0_ffn_Wv"], a["L0_ffn_Wo"],
        a["L0_ffn_gate_W"], a["L0_ffn_bq"][cols].T, a["L0_ffn_bk"][cols].T], axis=1)
    arrays["rows_w"] = np.ascontiguousarray(np.broadcast_to(np.concatenate([
        a["L0_ffn_bv"], a["L0_ffn_bo"], a["L0_ffn_ln1_g"], a["L0_ffn_ln1_b"], a["L0_ffn_gate_b"],
        a["L0_ffn_b2"].reshape(-1)]), (R, Q_END)))
    arrays["moe_w"] = np.concatenate([
        a["L0_ffn_W1"].transpose(1, 0, 2).reshape(D, -1),
        a["L0_ffn_W2"].reshape(NE, NC, 128, D).transpose(2, 0, 1, 3).reshape(128, -1),
        a["L0_ffn_b1"].reshape(NE * NC, 128).T], axis=1)

    p = np.arange(128)
    consts = np.zeros((128, C_END), f32)
    consts[:, C_ID:C_ID + 128] = np.eye(128)
    for t in range(NT):
        consts[p % 32 == t, C_BLK + t * R:C_BLK + (t + 1) * R] = -1.0
    consts[:, C_MHI] = p % 32 < 16
    consts[:, C_MLO] = p % 32 >= 16
    consts[:, C_ONE4] = p % 32 < NT
    consts[:, C_NLO] = -(p % 32 >= 16).astype(f32)
    consts[:, C_REV:C_END] = np.tile(NE - np.arange(NE), NT)
    arrays["consts"] = consts

    nc = _bacc.Bacc("TRN2", target_bir_lowering=False, num_devices=1)
    arrays = {f"in_{k}": np.ascontiguousarray(v) for k, v in arrays.items()}
    args = [nc.dram_tensor(f"in_{k}", arrays[f"in_{k}"].shape, F32, kind="ExternalInput").ap() for k in _IN]
    o = nc.dram_tensor("out", (B, S, D), F32, kind="ExternalOutput").ap()
    tower(nc, *args, o)
    r = _run(nc, [arrays], core_ids=[0])
    return r.results[0]["out"]
```

```python
from contextlib import ExitStack

import concourse.bass as bass
import numpy as np
from concourse import mybir

ALU = mybir.AluOpType
ACT = mybir.ActivationFunctionType
AX = mybir.AxisListType
F32 = mybir.dt.float32
F32R = mybir.dt.float32r
I32 = mybir.dt.int32

B, T, FIN, D, TAPS = 16, 500, 80, 128, 5
KIN = 96
S = T - TAPS + 1
NT = 4
R = S // NT
H1, E1 = 8, 64
H2, E2 = 8, 16
G2 = H2 // 4
NE, FF = 8, 512
NC = FF // 128
SEG = H1 * S // 128
N = B * S
TR, TC = 256, 2
MT = N // TR + NE
KT = -(-N // TR)
CAP = (KT + 1) * TR
PAY = 2 * D + 2
AHEAD = 8
NOBODY = 1 << 20
assert NT * R == S and H1 * S % 128 == 0
EPS = 1e-5
RSQRT_SEED = float(0x5F3759DF)
PADW = 640

C_ID, C_BLK, C_MHI, C_MLO, C_ONE4, C_NLO, C_REV = 0, 128, 624, 625, 626, 627, 632
C_UP = C_REV + NT * NE
C_ONES = C_UP + R
C_TOKEN = C_ONES + 128
C_REGION = C_TOKEN + NT
C_TILES = C_REGION + NE
C_TRI = C_TILES + NE * KT
C_WHICH = C_TRI + NE * NE
C_START = C_WHICH + MT * NE
C_END = C_START + MT

A_WQ, A_WK, A_WV, A_WLT = 0, 1024, 2048, 3072
A_END = 4096
P_WQ, P_WK, P_WV, P_WO, P_GW = 0, 256, 512, 640, 768
P_BQ, P_BK = 776, 778
P_END = 780
Q_BV, Q_BO, Q_G, Q_BETA, Q_GB = 0, 128, 256, 384, 512
Q_END = Q_GB + NE
N_W, N_B, N_GAMMA, N_BETA = 0, TAPS * D, TAPS * D + 1, TAPS * D + 2
N_END = TAPS * D + 3
M_W1, M_W2, M_B1, M_B2 = 0, FF, 2 * FF, 2 * FF + NC
M_END = M_B2 + D


def offset(h):
    return (h * S) % 128


def pieces(h):
    first = h * S // 128
    n = (offset(h) + S + 127) // 128
    return [(first + c, 128 * c, c > 0 or offset(h) == 0, c < n - 1 or (h + 1) * S % 128 == 0)
            for c in range(n)]


class Steps:

    def __init__(self, eng, sem):
        self.eng, self.sem, self.before, self.n = eng, sem, 0, 0

    def loop(self, i, per):
        self.outer, self.per = self.n, per
        self.before, self.n = i * per + self.outer, 0

    def end(self, trips):
        assert self.n == self.per, (self.n, self.per)
        self.before, self.n = 0, self.outer + trips * self.per

    def did(self, ins):
        ins.then_inc(self.sem, 1)
        self.n += 1

    def wait(self):
        self.eng.wait_ge(self.sem, self.before + self.n)


def tower(nc, xt, conv_w, att1_w, att2_w, rows_w, moe_w, pads, consts, routed, out):
    with ExitStack() as whole:
        def sem(name):
            return whole.enter_context(nc.semaphore(name))

        def sb(name, shape, dt=F32, ctx=whole):
            return ctx.enter_context(nc.sbuf_tensor(name, shape, dt))

        feat = sb("feat", [128, (B + 1) * S])
        toks = sb("toks", [128, B * NT * D])
        xin = toks[0:KIN, 0:B * T]
        resid = toks[0:R, :].rearrange("p (b n) -> p b n", b=B)
        cst = sb("cst", [128, C_END])
        ident = cst[:, C_ID:C_ID + 128]
        mask_hi, mask_lo = cst[:, C_MHI:C_MHI + 1], cst[:, C_MLO:C_MLO + 1]
        ones4 = cst[:, C_ONE4:C_ONE4 + 1]
        pad = sb("pad", [128, TC * PAY])
        rows = sb("rows", [R, Q_END])
        bn_st = sb("bn_st", [128, B, 6])
        bn_mv = sb("bn_mv", [128, 2])
        bn_s = sb("bn_s", [128, 4])
        ln1_st = sb("ln1_st", [R, B, NT * 6])
        ln1_mv = sb("ln1_mv", [R, B, NT * 2])
        ln1_t, ln1_v, ln1_r = (sb(n, [R, B * NT]) for n in ("ln1_t", "ln1_v", "ln1_r"))
        ln_st = sb("ln_st", [R, NT, 6])
        ln_mv = sb("ln_mv", [R, NT, 2])
        ln_v = sb("ln_v", [128, NT])
        ln_r = sb("ln_r", [128, NT])
        ln_t = sb("ln_t", [128, NT])
        ln_out = sb("ln_out", [R, NT, D])
        mx = sb("mx", [R, NT])
        qa = [sb(f"qa{i}", [128, S], F32R) for i in range(4)]
        qb = [sb(f"qb{i}", [128, S], F32R) for i in range(4)]
        val2 = sb("val2", [R, NT, H2, 32])
        zres = sb("zres", [128, S])
        o_tok = sb("o_tok", [R, NT, D])
        picks = sb("picks", [R, NT + 1, NE])
        w2a = sb("w2a", [128, P_END])
        runs_i = sb("runs_i", [1, NE], I32)
        table = sb("table", [1, 2, MT], I32)

        early = ExitStack()
        cw = sb("cw", [128, N_END], ctx=early)
        h1f = [sb(f"h1f{i}", [128, S], ctx=early) for i in range(2)]
        z1t = [sb(f"z1t{i}", [R, NT, D], ctx=early) for i in range(2)]
        early.close()

        a1 = ExitStack()
        prob = [sb(f"prob{i}", [R, NT, PADW], ctx=a1) for i in range(2)]
        w_hi = sb("w_hi", [128, A_WLT], F32R, ctx=a1)
        w_lo = sb("w_lo", [128, A_WLT], F32R, ctx=a1)
        wlt = sb("wlt", [128, H1, D], ctx=a1)
        z_hi = sb("z_hi", [128, S], F32R, ctx=a1)
        z_lo = sb("z_lo", [128, S], F32R, ctx=a1)
        xa, xb, ya, yb = ([sb(f"{n}{i}", [128, S], F32R, ctx=a1) for i in range(2)] for n in ("xa", "xb", "ya", "yb"))
        val = sb("val", [R, NT, H1, D + 1], ctx=a1)
        mixed = sb("mixed", [128, D * SEG], ctx=a1)
        raw = mixed[:, 0:A_WLT]
        rden = sb("rden", [128, (SEG + 2) // 3, 3], ctx=a1)
        a1.close()

        a2 = ExitStack()
        v_hi = sb("v_hi", [128, P_WV], F32R, ctx=a2)
        v_lo = sb("v_lo", [128, P_WV], F32R, ctx=a2)
        zc = sb("zc", [128, S], ctx=a2)
        zc_hi = sb("zc_hi", [128, S], F32R, ctx=a2)
        zc_lo = sb("zc_lo", [128, S], F32R, ctx=a2)
        q_hi = sb("q_hi", [128, S], F32R, ctx=a2)
        q_part = sb("q_part", [128, S], ctx=a2)
        k_part = sb("k_part", [128, S], ctx=a2)
        q_mix = sb("q_mix", [128, S], F32R, ctx=a2)
        side = sb("side", [128, 1 + 2 * G2], ctx=a2)
        ka = [sb(f"ka{i}", [128, S], F32R, ctx=a2) for i in range(2)]
        kb = [sb(f"kb{i}", [128, S], F32R, ctx=a2) for i in range(2)]
        prob2 = [sb(f"prob2_{i}", [R, NT, S], ctx=a2) for i in range(4)]
        o4 = sb("o4", [128, S], ctx=a2)
        rden2 = sb("rden2", [R, NT * 4], ctx=a2)
        o_feat = sb("o_feat", [128, S], ctx=a2)
        u = sb("u", [R, NT, D], ctx=a2)
        tc = sb("tc", [128, S], ctx=a2)
        lg = sb("lg", [R, NT, NE], ctx=a2)
        lmax = sb("lmax", [R, NT], ctx=a2)
        lexp = sb("lexp", [R, NT, NE], ctx=a2)
        lden = sb("lden", [R, NT], ctx=a2)
        pick = picks[:, 0:NT, :]
        place = sb("place", [R, NT, NE], ctx=a2)
        place_t = sb("place_t", [R, NT], ctx=a2)
        place_i = sb("place_i", [R, NT], I32, ctx=a2)
        token = sb("token", [R, NT], ctx=a2)
        pay = sb("pay", [R, NT, PAY], ctx=a2)
        runs = sb("runs", [R, NE], ctx=a2)
        cnt = sb("cnt", [1, NE], ctx=a2)
        more = sb("more", [1, NE, KT], ctx=a2)
        ntile = sb("ntile", [1, NE], ctx=a2)
        tri = sb("tri", [1, NE, NE], ctx=a2)
        upto = sb("upto", [1, NE], ctx=a2)
        past = sb("past", [1, MT, NE], ctx=a2)
        past_n = sb("past_n", [1, MT, NE], ctx=a2)
        whose = sb("whose", [1, MT], ctx=a2)
        before = sb("before", [1, MT], ctx=a2)
        a2.close()

        a3 = ExitStack()
        xr = [sb(f"xr{i}", [128, TC, PAY], ctx=a3) for i in range(AHEAD)]
        we = [sb(f"we{i}", [128, M_END], ctx=a3) for i in range(AHEAD)]
        xf = [sb(f"xf{i}", [128, TR], ctx=a3) for i in range(2)]
        hid = [sb(f"hid{i}", [128, NC, TR], ctx=a3) for i in range(2)]
        y = [sb(f"y{i}", [128, TC, D], ctx=a3) for i in range(2)]
        a3.close()

        ps = whole.enter_context(nc.psum_tensor("ps", [128, 8, 512], F32))
        sc = ps[:, 0:4, :]
        px, py, po = ps[:, 4, :], ps[:, 5, :], [ps[:, 6, :], ps[:, 7, :]]
        pair = [ps[:, 2 * i:2 * i + 2, :] for i in range(3)]
        pv, pm = ps[:, 6, :], ps[:, 7, :]
        ranks = pm[0:R, 128:128 + (NT + 1) * NE].rearrange("p (t n) -> p t n", t=NT + 1)

        def tiles(bank, w=D):
            return bank[0:R, 0:NT * w].rearrange("p (t n) -> p t n", t=NT)

        d_x = [sem(f"d_x{i}") for i in range(4)]
        d_cw, d_cst, d_a1, d_a2, d_rows = (sem(n) for n in ("d_cw", "d_cst", "d_a1", "d_a2", "d_rows"))
        d_routed, d_pad, d_fill = sem("d_routed"), sem("d_pad"), sem("d_fill")
        d_out = [sem("d_out0"), sem("d_out1")]
        d_tile = [sem(f"d_tile{i}") for i in range(AHEAD)]
        dve_step = sem("dve_step")
        held = sem("held")
        pool_step = sem("pool_step")
        conv_done, relu_done, stats_done, bn_ready = (sem(n) for n in ("conv_done", "relu_done", "stats_done", "bn_ready"))
        bn_applied, h1_turned, h1_kept, z1_ready, z1_turned, z1_kept = (sem(n) for n in (
            "bn_applied", "h1_turned", "h1_kept", "z1_ready", "z1_turned", "z1_kept"))
        w1_split, ones_set = sem("w1_split"), sem("ones_set")
        z_split, x_made, y_made, x_hi, y_hi, x_lo, y_lo = (sem(n) for n in (
            "z_split", "x_made", "y_made", "x_hi", "y_hi", "x_lo", "y_lo"))
        v_made, v_kept, s_made, max_done, max_turned, max_kept, st_made, exp_done = (sem(n) for n in (
            "v_made", "v_kept", "s_made", "max_done", "max_turned", "max_kept", "st_made", "exp_done"))
        pads_zero, seg_made, seg_kept, lt_made, h2_kept, z2_ready, z2_turned, z2_kept = (sem(n) for n in (
            "pads_zero", "seg_made", "seg_kept", "lt_made", "h2_kept", "z2_ready", "z2_turned", "z2_kept"))
        w2_split, z2_split, zc_ready, zres_ready, zeroed = (sem(n) for n in (
            "w2_split", "z2_split", "zc_ready", "zres_ready", "zeroed"))
        q_made, k_made, v2_made, q_hi_done, q_part_done, k_part_done, q_mixed, k_mixed, v2_kept, qa_done, qb_done = (
            sem(n) for n in ("q_made", "k_made", "v2_made", "q_hi_done", "q_part_done", "k_part_done", "q_mixed",
                             "k_mixed", "v2_kept", "qa_done", "qb_done"))
        ka_done = sem("ka_done")
        s2_made, max2_done, max2_turned, max2_kept, st2_made, exp2_done = (sem(n) for n in (
            "s2_made", "max2_done", "max2_turned", "max2_kept", "st2_made", "exp2_done"))
        o4_made, o4_kept, o4_turned, o_tok_done, of_turned, of_kept, wo_made, u_done = (sem(n) for n in (
            "o4_made", "o4_kept", "o4_turned", "o_tok_done", "of_turned", "of_kept", "wo_made", "u_done"))
        ln3_done, t_ready, t_turned, t_kept, lg_made, lg_done, lsub_done, lexp_done, pick_made = (sem(n) for n in (
            "ln3_done", "t_ready", "t_turned", "t_kept", "lg_made", "lg_done", "lsub_done", "lexp_done", "pick_made"))
        rank_made, rank_kept, placed, pay_res, table_made = (sem(n) for n in (
            "rank_made", "rank_kept", "placed", "pay_res", "table_made"))
        counted = sem("counted")
        xt_made, xt_kept, hid_made, gelu_done, y_moe_made, y_moe_used, y_done = (sem(n) for n in (
            "xt_made", "xt_kept", "hid_made", "gelu_done", "y_moe_made", "y_moe_used", "y_done"))

        USES = 4 * H2
        PAIR = [(u + 2) % 3 if u < USES - 2 else u % 3 for u in range(USES)]
        FIRST_USE = USES - 4

        def pair_free(pe, n, use):
            before = max(v for v in range(use - USES, use) if PAIR[v % USES] == PAIR[use])
            k, kind = before // 4, before % 4
            slot = use // 4
            head = n - (slot + (use % 4 < 2)) + k
            if kind < 2:
                pe.wait_ge(max2_done, 2 * (head + 1) + kind + 1)
            else:
                pe.wait_ge(exp2_done, 2 + 2 * head + kind - 1)

        def hold(eng):
            eng.sem_inc(held, 1)

        def arrived(i, k):
            return (i - k) * (32 // AHEAD) + 32

        def by_tile(eng, work, first=0, last=MT, step=None, per=0):
            rounds = last // AHEAD
            with eng.Fori(first // AHEAD, rounds) as r:
                if step:
                    step.loop(r - first // AHEAD, per * AHEAD)
                for k in range(AHEAD):
                    work(r * AHEAD + k, k, r * (AHEAD // 2) + k // 2)
                if step:
                    step.end(rounds - first // AHEAD)
            for k in range(last % AHEAD):
                work(rounds * AHEAD + k, k, rounds * (AHEAD // 2) + k // 2)

        def fill_regions(eng, experts):
            eng.wait_ge(counted, 1)
            for e in experts:
                end = eng.value_load(runs_i[0:1, e:e + 1], min_val=0, max_val=NE * CAP)
                eng.dma_start(routed[bass.ds(end, TR), :].rearrange("(p t) n -> p (t n)", t=TC), pad[:, :]).then_inc(d_fill, 16)

        def stored(eng, k, p):
            if not isinstance(p, int) or p:
                eng.wait_ge(d_out[k % 2], p * 16 * TC)

        def feat_b(b):
            return feat[:, bass.ds(b * S, S)]

        NSEG_GROUPS = (SEG + 2) // 3
        def parts(h):
            n = len(pieces(h))
            return 3, n - 1, n

        xw = w_hi[:, :].rearrange("p (w h n) -> p w h n", w=3, h=H1)
        xwl = w_lo[:, :].rearrange("p (w h n) -> p w h n", w=3, h=H1)

        def groups_in(h, a, b):
            return [w // 3 for w, _, _, last in pieces(h)[a:b] if last and (w % 3 == 2 or w == SEG - 1)]

        out_rows = out.rearrange("b s d -> (b s) d")

        block = whole.enter_context(nc.Block())

        @block.sync
        def _(sp):
            sp.dma_start(cw[:, :], conv_w).then_inc(d_cw, 16)
            for i in range(4):
                n = B * T // 4
                sp.dma_start(xin[:, i * n:(i + 1) * n], xt[:, i * n:(i + 1) * n]).then_inc(d_x[i], 16)
            sp.dma_start(cst[:, :], consts).then_inc(d_cst, 16)
            sp.dma_start(rows[:, :], rows_w).then_inc(d_rows, 16)
            sp.dma_start(raw, att1_w[:, 0:A_WLT]).then_inc(d_a1, 16)
            sp.dma_start(wlt[:, :, :].rearrange("p c n -> p (c n)"), att1_w[:, A_WLT:A_END]).then_inc(d_a1, 16)
            sp.dma_start(pad[:, :], pads).then_inc(d_pad, 16)
            sp.dma_start(w2a[:, :], att2_w).then_inc(d_a2, 16)
            sp.wait_ge(d_pad, 16)
            sp.dma_start(routed[NE * CAP:NE * CAP + TR, :].rearrange("(p t) n -> p (t n)", t=TC), pad[:, :]).then_inc(d_fill, 16)
            fill_regions(sp, range(NE // 2))

            def fetch_weights(i, k):
                whose_w = sp.value_load(table[0:1, 1, bass.ds(i, 1)], min_val=0, max_val=(NE - 1) * 128)
                sp.dma_start(we[k][:, :], moe_w[bass.ds(whose_w, 128), :]).then_inc(d_tile[k], 16)

            def fetch_rows(i, k):
                first = sp.value_load(table[0:1, 0, bass.ds(i, 1)], min_val=0, max_val=NE * CAP)
                sp.dma_start(xr[k][:, :, :].rearrange("p t n -> p (t n)"),
                             routed[bass.ds(first, TR), :].rearrange("(p t) n -> p (t n)", t=TC)).then_inc(d_tile[k], 16)

            sp.wait_ge(table_made, 1)
            sp.wait_ge(d_routed, 16 * NT * B)
            for i in range(AHEAD):
                fetch_weights(i, i)
                if i == 0:
                    sp.wait_ge(d_fill, 16 * (NE + 1))
                fetch_rows(i, i)

            def refill(i, k, p):
                sp.wait_ge(d_out[k % 2], (p - AHEAD // 2 + 1) * 16 * TC)
                fetch_rows(i, k)
                fetch_weights(i, k)

            by_tile(sp, refill, AHEAD)
            sp.wait_ge(d_out[0], (MT + 1) // 2 * 16 * TC)
            sp.wait_ge(d_out[1], MT // 2 * 16 * TC)

        @block.tensor
        def _(pe):
            for s in (h1_turned, z1_turned):
                pe.sem_inc(s, 2)
            pe.sem_inc(st2_made, 8)
            pe.sem_inc(y_moe_made, 2)
            pe.wait_ge(d_cw, 16)

            def conv(i):
                for k in range(2):
                    pe.wait_ge(relu_done, 2 + i * 2 + k - 1)
                    bank = (px, py)[k]
                    for tap in range(TAPS):
                        mm = pe.matmul(bank[:, 0:S], cw[0:KIN, N_W + tap * D:N_W + (tap + 1) * D],
                                       xin[:, bass.ds((i * 2 + k) * T + tap, S)],
                                       start=tap == 0, stop=tap == TAPS - 1)
                    mm.then_inc(conv_done, 1)

            for part in range(4):
                pe.wait_ge(d_x[part], 16)
                with pe.Fori(part * B // 8, (part + 1) * B // 8) as i:
                    conv(i)
            pe.wait_ge(d_cst, 16)

            def turn_h1(b, k):
                pe.wait_ge(bn_applied, b + 1)
                pe.wait_ge(h1_kept, 2 + b - 1)
                for t in range(NT):
                    mm = pe.transpose(tiles((px, py)[k])[:, t, :], h1f[k][:, t * R:(t + 1) * R], ident)
                mm.then_inc(h1_turned, 1)

            def turn_z1(b, k):
                pe.wait_ge(z1_ready, b + 1)
                pe.wait_ge(z1_kept, 2 + b - 1)
                for t in range(NT):
                    mm = pe.transpose(po[k][:, t * R:(t + 1) * R], z1t[k][:, t, :], ident[0:R, 0:R])
                mm.then_inc(z1_turned, 1)

            with pe.Fori(0, B // 2) as i:
                for k in range(2):
                    turn_h1(i * 2 + k, k)
            with pe.Fori(0, B // 2) as i:
                for k in range(2):
                    turn_z1(i * 2 + k, k)
            pe.wait_ge(w1_split, 2)
            pe.wait_ge(ones_set, 1)

            def split_product(dst, lhs_hi, lhs_lo, rhs_hi, rhs_lo):
                pe.matmul(dst, lhs_hi, rhs_lo, start=True, stop=False)
                pe.matmul(dst, lhs_lo, rhs_hi, start=False, stop=False)
                return pe.matmul(dst, lhs_hi, rhs_hi, start=False, stop=True)

            def project_y(h):
                split_product(py[:, 0:S], xw[:, 1, h, :], xwl[:, 1, h, :], z_hi[:, :], z_lo[:, :]).then_inc(y_made, 1)

            def project_x(h):
                split_product(px[:, 0:S], xw[:, 0, h, :], xwl[:, 0, h, :], z_hi[:, :], z_lo[:, :]).then_inc(x_made, 1)

            def values(b, i):
                t, half = i % NT, i // NT
                if i >= 2:
                    pe.wait_ge(v_kept, b * 8 + i - 1)
                w = slice(A_WV + 512 * half, A_WV + 512 * (half + 1))
                tok = slice(t * R, (t + 1) * R)
                split_product(po[i % 2][0:R, :], z_hi[:, tok], z_lo[:, tok], w_hi[:, w], w_lo[:, w]).then_inc(v_made, 1)

            def maxima(n, k):
                pe.wait_ge(x_hi, n + 1)
                pe.wait_ge(x_lo, n + 1)
                pe.wait_ge(y_hi, n + 1)
                for t in range(NT):
                    if t % 2 == 0:
                        pe.wait_ge(exp_done, 2 * n + t // 2 + 1)
                    mm = pe.matmul(sc[0:R, t, 0:S], xa[k][:, t * R:(t + 1) * R], ya[k][:, :], start=True, stop=True)
                mm.then_inc(s_made, 1)

            def turn_max(n):
                pe.wait_ge(max_done, n + 1)
                pe.matmul(px[64:64 + NT, 0:R], mx[:, :], ident[0:R, 0:R], start=True, stop=True).then_inc(max_turned, 1)

            def scores(n, k):
                pe.wait_ge(max_kept, n + 1)
                pe.wait_ge(y_lo, n + 1)
                for t in range(NT):
                    tok = slice(t * R, (t + 1) * R)
                    pe.matmul(sc[0:R, t, 0:S], yb[k][0:E1 + NT, tok], xb[k][0:E1 + NT, :], start=True, stop=False)
                    mm = pe.matmul(sc[0:R, t, 0:S], ya[k][:, tok], xa[k][:, :], start=False, stop=True)
                    if t % 2:
                        mm.then_inc(st_made, 1)

            def mix(b, h, first, last):
                todo = pieces(h)
                for w, col, opens, closes in todo[first:last]:
                    bank, at = po[w // 3 % 2], w % 3 * (D + 1)
                    if opens and w % 3 == 0 and w >= 6:
                        pe.wait_ge(seg_kept, b * NSEG_GROUPS + w // 3 - 1)
                    for t in range(NT):
                        mm = pe.matmul(bank[:, at:at + D + 1], prob[h % 2][:, t, col:col + 128], val[:, t, h, :],
                                       start=opens and t == 0, stop=closes and t == NT - 1)
                    if closes and (w % 3 == 2 or w == SEG - 1):
                        mm.then_inc(seg_made, 1)

            def project_out(b):
                pe.wait_ge(seg_kept, (b + 1) * NSEG_GROUPS)
                for t in range(NT):
                    for c in range(H1):
                        a = H1 * R * t + c
                        mm = pe.matmul(tiles(px)[:, t, :], mixed[:, a:a + H1 * (R - 1) + 1:H1], wlt[:, c, :],
                                       start=c == 0, stop=c == H1 - 1)
                mm.then_inc(lt_made, 1)

            def turn_z2(b):
                pe.wait_ge(z2_ready, b + 1)
                for t in range(NT):
                    mm = pe.transpose(py[:, t * R:(t + 1) * R], ln_out[:, t, :], ident[0:R, 0:R])
                mm.then_inc(z2_turned, 1)

            def row1(b, first):
                for h in range(H1):
                    n, mixes = b * H1 + h, h > 0 or not first
                    maxima(n, h % 2)
                    if h == 2 and not first:
                        pe.wait_ge(y_lo, n + 1)
                        turn_z2(b - 1)
                    if mixes:
                        pe.wait_ge(pads_zero, n)
                        if h == 1:
                            pe.wait_ge(v_kept, b * 8 + 8)
                        last_b, last_h = (b, h - 1) if h else (b - 1, H1 - 1)
                        a, c, n_parts = parts(last_h)
                        mix(last_b, last_h, 0, a)
                    if h == 1 and not first:
                        pe.wait_ge(h2_kept, b)
                    turn_max(n)
                    if mixes:
                        mix(last_b, last_h, a, c)
                    pe.wait_ge(y_lo, n + 1)
                    if h == 2 and not first:
                        pe.wait_ge(z2_kept, 1 + b)
                    if h == H1 - 1:
                        pe.wait_ge(z_split, b + 2)
                    project_y((h + 1) % H1)
                    pe.wait_ge(max_kept, n + 1)
                    project_x((h + 1) % H1)
                    scores(n, h % 2)
                    if mixes:
                        mix(last_b, last_h, c, n_parts)
                    if h == 0:
                        if not first:
                            pe.wait_ge(x_lo, n + 2)
                            project_out(b - 1)
                        for i in range(8):
                            values(b, i)

            pe.wait_ge(z_split, 1)
            project_y(0)
            project_x(0)
            row1(0, True)
            with pe.Fori(1, B) as b:
                row1(b, False)
            pe.wait_ge(exp_done, 2 * B * H1 + 2)
            pe.wait_ge(pads_zero, B * H1)
            mix(B - 1, H1 - 1, 0, 9)
            pe.wait_ge(x_lo, B * H1 + 1)
            pe.wait_ge(y_lo, B * H1 + 1)
            project_out(B - 1)
            turn_z2(B - 1)

            pe.wait_ge(w2_split, 2)
            pe.wait_ge(zeroed, 1)

            def values2(m, g):
                for t in range(NT):
                    mm = pe.matmul(tiles(pv, 64)[:, t, :], zc[:, t * R:(t + 1) * R],
                                   w2a[:, P_WV + 64 * g:P_WV + 64 * (g + 1)], start=True, stop=True)
                mm.then_inc(v2_made, 1)

            def project2(base, g, made):
                w = slice(base + 128 * g, base + 128 * (g + 1))
                split_product(pm[:, 0:S], v_hi[:, w], v_lo[:, w], zc_hi[:, :], zc_lo[:, :]).then_inc(made, 1)

            def maxima2(n, g, j, use, first=False):
                pe.wait_ge(qa_done, 1 + n + 1)
                for half in range(2):
                    if not first:
                        pair_free(pe, n, use + half)
                    for t in range(2):
                        tok = slice((2 * half + t) * R, (2 * half + t + 1) * R)
                        mm = pe.matmul(pair[PAIR[use + half]][0:R, t, 0:S], qa[j][:, tok], ka[g][:, :], start=True, stop=True)
                    mm.then_inc(s2_made, 1)

            def turn_max2(n, j):
                pe.wait_ge(max2_done, 2 * n + 2)
                pe.matmul(pm[32 * j:32 * j + NT, 0:R], mx[:, :], ident[0:R, 0:R], start=True, stop=True,
                          tile_position=(0, 32 * j)).then_inc(max2_turned, 1)

            def scores2(n, g, j, use):
                pe.wait_ge(max2_kept, n + 1)
                for half in range(2):
                    pair_free(pe, n, use + half)
                    for t in range(2):
                        tok = slice((2 * half + t) * R, (2 * half + t + 1) * R)
                        dst = pair[PAIR[use + half]][0:R, t, 0:S]
                        pe.matmul(dst, kb[g][:, tok], qb[j][:, :], start=True, stop=False)
                        mm = pe.matmul(dst, ka[g][:, tok], qa[j][:, :], start=False, stop=True)
                    mm.then_inc(st2_made, 1)

            def mix2(m, g):
                if isinstance(m, int) and m == 0:
                    pe.matmul(pv[:, 0:S], cst[:, C_ONES:C_ONES + 128], cst[:, C_BLK:C_BLK + S], start=True,
                              stop=True).then_inc(o4_made, 1)
                    return
                pe.wait_ge(exp2_done, 2 + m * 8)
                pe.wait_ge(v2_kept, 1 + m)
                for t in range(NT):
                    for j in range(4):
                        mm = pe.matmul(pv[32 * j:32 * j + 32, 0:S], val2[:, t, 4 * g + j, :], prob2[j][:, t, :],
                                       start=t == 0, stop=t == NT - 1, tile_position=(0, 32 * j))
                mm.then_inc(o4_made, 1)

            def turn_o4(m):
                pe.wait_ge(o4_kept, m + 1)
                for t in range(NT):
                    mm = pe.transpose(tiles(pv)[:, t, :], o4[:, t * R:(t + 1) * R], ident)
                mm.then_inc(o4_turned, 1)

            def turn_o(m):
                pe.wait_ge(o_tok_done, m + 1)
                for t in range(NT):
                    mm = pe.transpose(pv[:, t * R:(t + 1) * R], o_tok[:, t, :], ident[0:R, 0:R])
                mm.then_inc(of_turned, 1)

            def out_product(b):
                pe.wait_ge(of_kept, b + 1)
                pe.wait_ge(zres_ready, 1 + b)
                for t in range(NT):
                    tok = slice(t * R, (t + 1) * R)
                    pe.matmul(tiles(pv)[:, t, :], zres[:, tok], ident, start=True, stop=False)
                    mm = pe.matmul(tiles(pv)[:, t, :], o_feat[:, tok], w2a[:, P_WO:P_WO + D], start=False, stop=True)
                mm.then_inc(wo_made, 1)

            def turn_t(b):
                pe.wait_ge(t_ready, b + 1)
                for t in range(NT):
                    mm = pe.transpose(pv[:, t * R:(t + 1) * R], pay[:, t, 0:D], ident[0:R, 0:R])
                mm.then_inc(t_turned, 1)

            def logits(b):
                pe.wait_ge(t_kept, b + 1)
                for t in range(NT):
                    mm = pe.matmul(tiles(pv, NE)[:, t, :], tc[:, t * R:(t + 1) * R], w2a[:, P_GW:P_GW + NE],
                                   start=True, stop=True)
                mm.then_inc(lg_made, 1)

            def rank(b):
                pe.wait_ge(pick_made, b)
                above, ones = cst[0:R, C_UP:C_UP + R], cst[0:R, C_ONES:C_ONES + R]
                pe.matmul(ranks[:, :, :], above, picks[:, :, :], start=True, stop=False)
                for t in range(NT):
                    mm = pe.matmul(ranks[:, t + 1:, :], ones, pick[:, t:t + 1, :].broadcast_to([R, NT - t, NE]),
                                   start=False, stop=t == NT - 1)
                mm.then_inc(rank_made, 1)

            pe.wait_ge(z2_split, 1)
            pe.wait_ge(zc_ready, 1)
            values2(0, 0)
            project2(P_WQ, 0, q_made)
            pe.wait_ge(q_mixed, 1)
            project2(P_WK, 0, k_made)
            pe.wait_ge(k_mixed, 1)
            pe.wait_ge(v2_kept, 2)
            maxima2(0, 0, 0, FIRST_USE, first=True)

            def row2(b, routes):
                for g in range(G2):
                    m, other = b * G2 + g, 1 - g
                    for j in range(4):
                        n, use = b * H2 + 4 * g + j, 4 * (4 * g + j)
                        if j == 1 and g == 0 and routes:
                            pe.wait_ge(rank_kept, b - 1)
                        if j == 2:
                            pe.wait_ge(q_mixed, m + 2)
                        if j == 3:
                            pe.wait_ge(k_mixed, m + 2)
                        turn_max2(n, j)
                        maxima2(n + 1, g if j < 3 else other, (j + 1) % 4, use)
                        if j == 0:
                            if g == 0:
                                pe.wait_ge(lg_done, 1 + b)
                            else:
                                pe.wait_ge(u_done, b + 1)
                            mix2(m, other)
                        if j == 1:
                            if g == 1:
                                pe.wait_ge(zc_ready, b + 2)
                                pe.wait_ge(z2_split, b + 2)
                            pe.wait_ge(max2_kept, n + 1)
                            project2(P_WQ, other, q_made)
                            pe.wait_ge(o_tok_done, m + 1)
                            values2(m + 1, other)
                        if j == 2:
                            pe.wait_ge(max2_kept, n + 1)
                            project2(P_WK, other, k_made)
                        scores2(n, g, j, use + 2)
                        if j == 0 and g == 0 and routes:
                            rank(b)
                        if j == 0:
                            turn_o4(m)
                        if j == 1:
                            pe.wait_ge(v2_kept, m + 3)
                            if g == 0:
                                turn_o(m)
                        if j == 2:
                            if g == 0:
                                out_product(b)
                            else:
                                turn_t(b)
                        if j == 3 and g == 1:
                            logits(b)

            row2(0, False)
            row2(1, False)
            with pe.Fori(2, B) as b:
                row2(b, True)
            pe.wait_ge(lg_done, 1 + B)
            mix2(B * G2, 1)
            rank(B)
            turn_o4(B * G2)
            turn_o(B * G2)
            out_product(B)
            pe.wait_ge(u_done, B + 1)
            turn_t(B)
            logits(B)
            pe.wait_ge(rank_kept, B - 1)
            rank(B + 1)

            def turn_x(i, k):
                pe.wait_ge(d_tile[k], arrived(i, k))
                pe.wait_ge(xt_kept, 2 + i - 1)
                for t in range(TC):
                    mm = pe.transpose((px, py)[k % 2][:, t * 128:(t + 1) * 128], xr[k][:, t, 0:D], ident)
                mm.then_inc(xt_made, 1)

            def up(i, k):
                pe.wait_ge(xt_kept, 2 + i + 1)
                for c in range(NC):
                    pe.wait_ge(gelu_done, NC + i * NC + c - (NC - 1))
                    pe.matmul(sc[:, c, 0:TR], we[k][:, M_W1 + c * 128:M_W1 + (c + 1) * 128], xf[k % 2][:, :], start=True,
                              stop=True).then_inc(hid_made, 1)

            def down(i, k):
                pe.wait_ge(gelu_done, NC + (i + 1) * NC)
                pe.wait_ge(y_moe_used, 2 + i - 1)
                for t in range(TC):
                    for c in range(NC):
                        mm = pe.matmul(po[k % 2][:, t * D:(t + 1) * D], hid[k % 2][:, c, t * 128:(t + 1) * 128],
                                       we[k][:, M_W2 + c * 128:M_W2 + (c + 1) * 128], start=c == 0, stop=c == NC - 1)
                mm.then_inc(y_moe_made, 1)

            turn_x(0, 0)
            up(0, 0)
            turn_x(1, 1)

            def tile(i, k, p):
                up(i + 1, (k + 1) % AHEAD)
                turn_x(i + 2, (k + 2) % AHEAD)
                down(i, k)

            by_tile(pe, tile, last=MT - 2)
            up(MT - 1, (MT - 1) % AHEAD)
            down(MT - 2, (MT - 2) % AHEAD)
            down(MT - 1, (MT - 1) % AHEAD)

        @block.scalar
        def _(act):
            for s in (relu_done, h1_kept, z1_kept):
                act.sem_inc(s, 2)
            for s in (z2_kept, qa_done):
                act.sem_inc(s, 1)
            act.sem_inc(exp_done, 2)
            act.sem_inc(exp2_done, 2)
            act.sem_inc(gelu_done, NC)
            act.wait_ge(d_cw, 16)
            act.wait_ge(d_cst, 16)
            with act.Fori(0, B // 2) as i:
                for k, bank in enumerate((px, py)):
                    act.wait_ge(conv_done, i * 2 + k + 1)
                    act.activation(feat_b(i * 2 + k), bank[:, 0:S], ACT.Relu, bias=cw[:, N_B:N_B + 1]).then_inc(relu_done, 1)
            act.wait_ge(bn_ready, 1)

            def norm_h1(b, k):
                act.wait_ge(h1_turned, 2 + b - 1)
                act.activation(h1f[k][:, :], feat_b(b), ACT.Identity, bias=bn_s[:, 3:4], scale=bn_s[:, 2:3]).then_inc(bn_applied, 1)

            def keep_h1(b, k):
                act.wait_ge(h1_turned, 2 + b + 1)
                hold(act)
                act.copy(resid[:, bass.ds(b, 1), :].rearrange("p a n -> p (a n)"), (px, py)[k][0:R, :]).then_inc(h1_kept, 1)

            def keep_z1(b, k):
                act.wait_ge(z1_turned, 2 + b + 1)
                hold(act)
                act.copy(feat_b(b), po[k][:, 0:S]).then_inc(z1_kept, 1)

            norm_h1(0, 0)
            with act.Fori(0, B // 2 - 1) as i:
                for k in range(2):
                    norm_h1(i * 2 + k + 1, 1 - k)
                    keep_h1(i * 2 + k, k)
            norm_h1(B - 1, 1)
            keep_h1(B - 2, 0)
            keep_h1(B - 1, 1)
            with act.Fori(0, B // 2) as i:
                for k in range(2):
                    keep_z1(i * 2 + k, k)

            def high_parts(n, k):
                act.wait_ge(y_made, n + 1)
                act.copy(ya[k][:, :], py[:, 0:S]).then_inc(y_hi, 1)
                act.wait_ge(x_made, n + 1)
                act.copy(xb[k][:, :], px[:, 0:S])
                act.copy(xa[k][0:E1, :], px[0:E1, 0:S]).then_inc(x_hi, 1)

            def exps1(n, h):
                for half in range(2):
                    act.wait_ge(st_made, 2 * n + half + 1)
                    act.activation(prob[h % 2][:, 2 * half:2 * half + 2, offset(h):offset(h) + S],
                                   sc[0:R, 2 * half:2 * half + 2, 0:S], ACT.Exp, scale=1.0 / E1).then_inc(exp_done, 1)

            def keep_z2(b):
                act.wait_ge(z2_turned, b + 1)
                hold(act)
                act.copy(feat_b(b), py[:, 0:S]).then_inc(z2_kept, 1)

            def row1(b, first):
                for h in range(H1):
                    if h == 2 and not first:
                        keep_z2(b - 1)
                    high_parts(b * H1 + h + 1, (h + 1) % 2)
                    exps1(b * H1 + h, h)
                    if h == 0:
                        for i in range(8):
                            act.wait_ge(v_made, b * 8 + i + 1)
                            t, half = i % NT, i // NT
                            act.copy(val[:, t, 4 * half:4 * half + 4, 0:D],
                                     po[i % 2][0:R, :].rearrange("p (h n) -> p h n", h=4)).then_inc(v_kept, 1)

            high_parts(0, 0)
            row1(0, True)
            with act.Fori(1, B) as b:
                row1(b, False)
            keep_z2(B - 1)

            act.wait_ge(d_a2, 16)
            act.wait_ge(zeroed, 1)
            act.wait_ge(w2_split, 2)

            def q_high(m, g):
                act.wait_ge(q_made, m + 1)
                act.wait_ge(qb_done, 4 + m * 4)
                act.activation(q_hi[:, :], pm[:, 0:S], ACT.Identity, bias=w2a[:, P_BQ + g:P_BQ + g + 1]).then_inc(q_hi_done, 1)
                act.wait_ge(q_hi_done, m + 1)
                act.activation(q_part[:, :], q_hi[:, :].bitcast(F32), ACT.Identity, bias=side[:, 1 + g:2 + g],
                               scale=side[:, 0:1]).then_inc(q_part_done, 1)

            def k_high(m, g):
                act.wait_ge(k_made, m + 1)
                act.activation(ka[g][:, :], pm[:, 0:S], ACT.Identity, bias=w2a[:, P_BK + g:P_BK + g + 1]).then_inc(ka_done, 1)
                act.wait_ge(ka_done, m + 1)
                act.activation(k_part[:, :], ka[g][:, :].bitcast(F32), ACT.Identity, bias=side[:, 3 + g:4 + g],
                               scale=cst[:, C_NLO:C_NLO + 1]).then_inc(k_part_done, 1)

            def keep_qa(m, j):
                rows_j = slice(32 * j, 32 * j + 32)
                act.wait_ge(q_mixed, m + 1)
                act.wait_ge(st2_made, m * 8 + 2 * j + 2)
                act.copy(qa[j][rows_j, :], q_mix[rows_j, :].bitcast(F32)).then_inc(qa_done, 1)

            def exps(n, j, use):
                for half in range(2):
                    act.wait_ge(st2_made, 8 + 2 * n + half + 1)
                    act.activation(prob2[j][:, 2 * half:2 * half + 2, :], pair[PAIR[use + half]][0:R, :, 0:S], ACT.Exp,
                                   scale=float(E2) ** -0.5).then_inc(exp2_done, 1)

            def keep_o4(m):
                act.wait_ge(o4_made, m + 1)
                act.copy(o4[:, :], pv[:, 0:S]).then_inc(o4_kept, 1)

            def keep_of(b):
                act.wait_ge(of_turned, b + 1)
                act.copy(o_feat[:, :], pv[:, 0:S]).then_inc(of_kept, 1)

            def keep_t(b):
                act.wait_ge(t_turned, b + 1)
                act.copy(tc[:, :], pv[:, 0:S]).then_inc(t_kept, 1)

            def exp_logits(b):
                act.wait_ge(lsub_done, b + 1)
                act.activation(lexp[:, :, :], lg[:, :, :], ACT.Exp).then_inc(lexp_done, 1)

            q_high(0, 0)
            k_high(0, 0)
            for j in range(3):
                keep_qa(0, j)

            def row2(b):
                for g in range(G2):
                    m, n, other = b * G2 + g, b * H2 + 4 * g, 1 - g
                    use = [4 * (4 * g + j) + 2 for j in range(4)]
                    keep_qa(m, 3)
                    keep_o4(m)
                    exps(n, 0, use[0])
                    q_high(m + 1, other)
                    exps(n + 1, 1, use[1])
                    if g == 0:
                        keep_of(b)
                    k_high(m + 1, other)
                    keep_qa(m + 1, 0)
                    exps(n + 2, 2, use[2])
                    keep_qa(m + 1, 1)
                    if g == 1:
                        keep_t(b)
                    exps(n + 3, 3, use[3])
                    keep_qa(m + 1, 2)
                    if g == 1:
                        exp_logits(b)

            row2(0)
            row2(1)
            with act.Fori(2, B) as b:
                row2(b)
            keep_o4(B * G2)
            keep_of(B)
            keep_t(B)
            exp_logits(B)

            fill_regions(act, range(NE // 2, NE))

            def hidden(i, k, p):
                act.wait_ge(y_moe_made, 2 + i - 1)
                for c in range(NC):
                    act.wait_ge(hid_made, i * NC + c + 1)
                    act.activation(hid[k % 2][:, c, :], sc[:, c, 0:TR], ACT.Gelu_apprx_tanh,
                                   bias=we[k][:, M_B1 + c:M_B1 + c + 1]).then_inc(gelu_done, 1)

            by_tile(act, hidden)

        @block.vector
        def _(dve):
            for s in (v2_kept, lg_done, zres_ready):
                dve.sem_inc(s, 1)
            for s in (xt_kept, y_moe_used):
                dve.sem_inc(s, 2)
            step = Steps(dve, dve_step)

            dve.wait_ge(d_a1, 32)
            step.did(dve.tensor_copy(w_hi[:, :], raw))
            step.wait()
            dve.tensor_tensor(w_lo[:, :], raw, w_hi[:, :].bitcast(F32), ALU.subtract).then_inc(w1_split, 2)

            def rsqrt(out_, var, scratch, v, first=0, last=3):
                if first == 0:
                    rsqrt_seed(out_, var, v)
                for _ in range(first, last):
                    step.did(dve.scalar_tensor_tensor(out=scratch, in0=out_, scalar=-0.5, in1=out_, op0=ALU.mult, op1=ALU.mult))
                    step.wait()
                    step.did(dve.tensor_tensor(scratch, scratch, v, ALU.mult))
                    step.wait()
                    step.did(dve.scalar_tensor_tensor(out=out_, in0=scratch, scalar=1.5, in1=out_, op0=ALU.add, op1=ALU.mult))
                    step.wait()

            def rsqrt_seed(out_, var, v):
                step.did(dve.tensor_scalar(v, var, EPS, None, ALU.add))
                step.wait()
                step.did(dve.tensor_scalar(out_.bitcast(I32), v.bitcast(I32), -0.5, RSQRT_SEED, ALU.mult, ALU.add))
                step.wait()

            def ln_start(src, newton):
                hold(dve)
                for t in range(NT):
                    st = dve.bn_stats(ln_st[:, t, :], src[:, t, :])
                step.did(st)
                step.wait()
                hold(dve)
                for t in range(NT):
                    st = dve.bn_aggr(ln_mv[:, t, :], ln_st[:, t, :])
                step.did(st)
                step.wait()
                rsqrt(ln_r[0:R, :], ln_mv[:, :, 1], ln_t[0:R, :], ln_v[0:R, :], last=newton)

            def ln_end(src, dst, newton):
                rsqrt(ln_r[0:R, :], ln_mv[:, :, 1], ln_t[0:R, :], ln_v[0:R, :], first=newton)
                for t in range(NT):
                    last = dve.tensor_scalar(dst[:, t, :], src[:, t, :], ln_mv[:, t, 0:1], ln_r[0:R, t:t + 1],
                                             ALU.subtract, ALU.mult)
                return last

            def layer_norm(src, dst=ln_out):
                ln_start(src, 3)
                return ln_end(src, dst, 3)

            LN_STEPS = 13

            dve.wait_ge(d_cst, 16)
            with dve.Fori(0, B) as b:
                dve.wait_ge(relu_done, 2 + b + 1)
                hold(dve)
                dve.bn_stats(bn_st[:, bass.ds(b, 1), :].rearrange("p a n -> p (a n)"), feat_b(b)).then_inc(stats_done, 1)
            dve.wait_ge(stats_done, B)
            step.did(dve.bn_aggr(bn_mv[:, :], bn_st[:, :, :]))
            step.wait()
            rsqrt(bn_s[:, 0:1], bn_mv[:, 1:2], bn_s[:, 1:2], ln_v[:, 0:1])
            dve.wait_ge(d_cw, 16)
            step.did(dve.tensor_tensor(bn_s[:, 2:3], bn_s[:, 0:1], cw[:, N_GAMMA:N_GAMMA + 1], ALU.mult))
            step.wait()
            step.did(dve.tensor_tensor(bn_s[:, 1:2], bn_s[:, 2:3], bn_mv[:, 0:1], ALU.mult))
            step.wait()
            dve.tensor_tensor(bn_s[:, 3:4], cw[:, N_BETA:N_BETA + 1], bn_s[:, 1:2], ALU.subtract).then_inc(bn_ready, 1)

            with dve.Fori(0, B) as b:
                step.loop(b, 1)
                dve.wait_ge(h1_kept, 2 + b + 1)
                hold(dve)
                for t in range(NT):
                    st = dve.bn_stats(ln1_st[:, bass.ds(b, 1), 6 * t:6 * t + 6].rearrange("p a n -> p (a n)"),
                                      resid[:, bass.ds(b, 1), t * D:(t + 1) * D].rearrange("p a n -> p (a n)"))
                step.did(st)
                step.end(B)
            step.wait()
            for b in range(B):
                for t in range(NT):
                    st = dve.bn_aggr(ln1_mv[:, b, 2 * t:2 * t + 2], ln1_st[:, b, 6 * t:6 * t + 6])
            step.did(st)
            step.wait()
            mv = ln1_mv[:, :, :].rearrange("p b (t n) -> p (b t) n", n=2)
            rsqrt(ln1_r[:, :], mv[:, :, 1], ln1_t[:, :], ln1_v[:, :])
            ln1_rb = ln1_r[:, :].rearrange("p (b t) -> p b t", b=B)
            with dve.Fori(0, B // 2) as i:
                for k in range(2):
                    b = i * 2 + k
                    dve.wait_ge(z1_turned, 2 + b - 1)
                    hold(dve)
                    for t in range(NT):
                        last = dve.tensor_scalar(z1t[k][:, t, :], resid[:, bass.ds(b, 1), t * D:(t + 1) * D].rearrange("p a n -> p (a n)"),
                                                 ln1_mv[:, bass.ds(b, 1), 2 * t:2 * t + 1].rearrange("p a n -> p (a n)"),
                                                 ln1_rb[:, bass.ds(b, 1), t:t + 1].rearrange("p a n -> p (a n)"),
                                                 ALU.subtract, ALU.mult)
                    last.then_inc(z1_ready, 1)

            def split_z1(b):
                step.did(dve.tensor_copy(z_hi[:, :], feat_b(b)))
                step.wait()
                dve.tensor_tensor(z_lo[:, :], feat_b(b), z_hi[:, :].bitcast(F32), ALU.subtract).then_inc(z_split, 1)

            def low_parts(n, k):
                dve.wait_ge(y_hi, n + 1)
                dve.tensor_tensor(yb[k][0:E1, :], py[0:E1, 0:S], ya[k][0:E1, :].bitcast(F32), ALU.subtract).then_inc(y_lo, 1)
                dve.wait_ge(x_hi, n + 1)
                dve.tensor_tensor(xa[k][E1:128, :], px[E1:128, 0:S], xb[k][E1:128, :].bitcast(F32), ALU.subtract).then_inc(x_lo, 1)

            def keep_group(b, q):
                n = min(3, SEG - 3 * q)
                src = po[q % 2][:, 0:n * (D + 1)].rearrange("p (j n) -> p j n", j=n)
                dve.wait_ge(seg_made, b * NSEG_GROUPS + q + 1)
                step.did(dve.reciprocal(rden[:, q, 0:n], src[:, :, D]))
                step.wait()
                dst = mixed[:, :].rearrange("p (f w) -> p w f", w=SEG)[:, 3 * q:3 * q + n, :]
                dve.tensor_tensor(dst, src[:, :, 0:D], rden[:, q, 0:n].unsqueeze(2).broadcast_to([128, n, D]),
                                  ALU.mult).then_inc(seg_kept, 1)

            def keep_max(rows_, bank, dst, b_h, turned, kept):
                dve.wait_ge(turned, b_h + 1)
                dve.tensor_tensor(dst[rows_, :].rearrange("p (t n) -> p t n", t=NT),
                                  bank[rows_, 0:R].unsqueeze(1).broadcast_to([NT, NT, R]),
                                  cst[rows_, C_BLK:C_BLK + S].rearrange("p (t n) -> p t n", t=NT),
                                  ALU.mult).then_inc(kept, 1)

            def end1(b):
                rb = resid[:, bass.ds(b, 1), :].rearrange("p a n -> p (a n)")
                dve.wait_ge(lt_made, b + 1)
                dve.tensor_tensor(rb, rb, px[0:R, :], ALU.add).then_inc(h2_kept, 1)
                dve.wait_ge(h2_kept, b + 1)
                layer_norm(resid[:, bass.ds(b, 1), :].rearrange("p a (t n) -> p (a t) n", t=NT)).then_inc(z2_ready, 1)

            def row1(b, first):
                for h in range(H1):
                    n, mixes = b * H1 + h, h > 0 or not first
                    last_b, last_h = (b, h - 1) if h else (b - 1, H1 - 1)
                    dve.wait_ge(s_made, n + 1)
                    dve.tensor_reduce(mx[:, :], sc[0:R, :, 0:S], AX.X, ALU.max).then_inc(max_done, 1)
                    keep_max(slice(64, 64 + NT), px, xb[h % 2], n, max_turned, max_kept)
                    if mixes:
                        for q in groups_in(last_h, 0, parts(last_h)[1]):
                            keep_group(last_b, q)
                    low_parts(n + 1, (h + 1) % 2)
                    if mixes:
                        for q in groups_in(last_h, *parts(last_h)[1:]):
                            keep_group(last_b, q)
                    if h == H1 - 2:
                        split_z1(b + 1)
                    if h == 0 and not first:
                        end1(b - 1)

            split_z1(0)
            low_parts(0, 0)
            row1(0, True)
            with dve.Fori(1, B) as b:
                step.loop(b - 1, 1 + NSEG_GROUPS + LN_STEPS)
                row1(b, False)
                step.end(B - 1)
            for q in groups_in(H1 - 1, 0, 9):
                keep_group(B - 1, q)
            end1(B - 1)

            dve.wait_ge(d_a2, 16)
            dve.wait_ge(d_rows, 16)
            step.did(dve.tensor_copy(v_hi[:, :], w2a[:, 0:P_WV]))
            step.wait()
            dve.tensor_scalar(side[:, 1:3], w2a[:, P_BQ:P_BQ + 2], mask_lo, None, ALU.mult)
            dve.tensor_scalar(side[:, 3:5], w2a[:, P_BK:P_BK + 2], mask_lo, ones4, ALU.mult, ALU.add)
            dve.tensor_tensor(side[:, 0:1], mask_hi, mask_lo, ALU.subtract)
            dve.tensor_tensor(v_lo[:, :], w2a[:, 0:P_WV], v_hi[:, :].bitcast(F32), ALU.subtract).then_inc(w2_split, 2)
            dve.wait_ge(zeroed, 1)

            def row(c, n=D):
                return rows[:, c:c + n].unsqueeze(1).broadcast_to([R, NT, n])

            def many(a):
                return a.unsqueeze(2).broadcast_to([R, NT, NE])

            def mix_q(m):
                dve.wait_ge(q_part_done, m + 1)
                dve.wait_ge(qa_done, 1 + m * 4)
                dve.scalar_tensor_tensor(out=q_mix[:, :], in0=pm[:, 0:S], scalar=mask_lo, in1=q_part[:, :],
                                         op0=ALU.mult, op1=ALU.add).then_inc(q_mixed, 1)

            def mix_k(m, g):
                dve.wait_ge(k_part_done, m + 1)
                dve.scalar_tensor_tensor(out=kb[g][:, :], in0=pm[:, 0:S], scalar=mask_lo, in1=k_part[:, :],
                                         op0=ALU.mult, op1=ALU.add).then_inc(k_mixed, 1)

            def keep_v2(m, g):
                dve.wait_ge(v2_made, m + 1)
                dve.tensor_tensor(val2[:, :, 4 * g:4 * g + 4, 0:E2],
                                  tiles(pv, 64).rearrange("p t (h n) -> p t h n", h=4),
                                  rows[:, Q_BV + 64 * g:Q_BV + 64 * (g + 1)].rearrange("p (h n) -> p h n", h=4)
                                  .unsqueeze(1).broadcast_to([R, NT, 4, E2]), ALU.add).then_inc(v2_kept, 1)

            def maxima2(n, use):
                for half in range(2):
                    dve.wait_ge(s2_made, 2 * n + half + 1)
                    dve.tensor_reduce(mx[:, 2 * half:2 * half + 2], pair[PAIR[use + half]][0:R, :, 0:S], AX.X,
                                      ALU.max).then_inc(max2_done, 1)

            def norm_o(m, g):
                dve.wait_ge(o4_turned, m + 1)
                o_in = tiles(pv).rearrange("p t (j n) -> p t j n", j=4)
                step.did(dve.reciprocal(rden2[:, :].rearrange("p (t j) -> p t j", t=NT), o_in[:, :, :, E2]))
                step.wait()
                dve.tensor_tensor(o_tok[:, :, 64 * g:64 * (g + 1)].rearrange("p t (j n) -> p t j n", j=4),
                                  o_in[:, :, :, 0:E2],
                                  rden2[:, :].rearrange("p (t j) -> p t j", t=NT).unsqueeze(3).broadcast_to([R, NT, 4, E2]),
                                  ALU.mult).then_inc(o_tok_done, 1)

            def add_bias(b):
                dve.wait_ge(wo_made, b + 1)
                dve.tensor_tensor(u[:, :, :], tiles(pv), row(Q_BO), ALU.add).then_inc(u_done, 1)

            def norm_u(b):
                dve.wait_ge(u_done, b + 1)
                ln_start(u, 1)

            def norm_u_roots(b):
                step.wait()
                rsqrt(ln_r[0:R, :], ln_mv[:, :, 1], ln_t[0:R, :], ln_v[0:R, :], first=1)

            def norm_u_end(b):
                step.wait()
                ln_end(u, ln_out, 3).then_inc(ln3_done, 1)

            def gate_start(b):
                dve.wait_ge(lg_made, b + 1)
                dve.tensor_tensor(lg[:, :, :], tiles(pv, NE), row(Q_GB, NE), ALU.add).then_inc(lg_done, 1)
                dve.wait_ge(lg_done, 1 + b + 1)
                step.did(dve.tensor_reduce(lmax[:, :], lg[:, :, :], AX.X, ALU.max))
                step.wait()
                dve.tensor_tensor(lg[:, :, :], lg[:, :, :], many(lmax[:, :]), ALU.subtract).then_inc(lsub_done, 1)

            def gate_end(b):
                rev = cst[0:R, C_REV:C_REV + NT * NE].rearrange("p (t n) -> p t n", t=NT)
                dve.wait_ge(lsub_done, b + 1)
                step.did(dve.scalar_tensor_tensor(out=pick[:, :, :], in0=lg[:, :, :], scalar=0.0, in1=rev, op0=ALU.is_equal, op1=ALU.mult))
                step.wait()
                step.did(dve.tensor_reduce(lmax[:, :], pick[:, :, :], AX.X, ALU.max))
                dve.wait_ge(lexp_done, b + 1)
                step.did(dve.tensor_reduce(lden[:, :], lexp[:, :, :], AX.X, ALU.add))
                step.wait()
                dve.tensor_tensor(pick[:, :, :], pick[:, :, :], many(lmax[:, :]), ALU.is_equal).then_inc(pick_made, 1)
                step.did(dve.reciprocal(lden[:, :], lden[:, :]))

            pay_i = pay[:, :, :].bitcast(I32)

            def route(b):
                dve.wait_ge(rank_made, b - 1)
                step.did(dve.tensor_tensor(place[:, :, :], ranks[:, 0:NT, :], runs[:, :].unsqueeze(1).broadcast_to([R, NT, NE]), ALU.add))
                step.wait()
                dve.tensor_tensor(runs[:, :], runs[:, :], ranks[:, NT, :], ALU.add).then_inc(rank_kept, 1)

            def label(b):
                dve.wait_ge(rank_kept, b - 1)
                step.did(dve.tensor_tensor(place[:, :, :], place[:, :, :], pick[:, :, :], ALU.mult))
                step.wait()
                step.did(dve.tensor_reduce(place_t[:, :], place[:, :, :], AX.X, ALU.add))
                step.wait()
                dve.wait_ge(t_ready, b)
                dve.tensor_copy(place_i[:, :], place_t[:, :])
                dve.tensor_copy(pay[:, :, 2 * D], lden[:, :])
                dve.tensor_copy(pay_i[:, :, 2 * D + 1], token[:, :]).then_inc(placed, 1)
                dve.wait_ge(placed, b - 1)
                step.did(dve.tensor_scalar(token[:, :], token[:, :], float(S), None, ALU.add))
                step.wait()

            step.did(dve.tensor_copy(token[:, :], cst[0:R, C_TOKEN:C_TOKEN + NT]))
            step.did(dve.tensor_copy(runs[:, :], cst[0:R, C_REGION:C_REGION + NE]))
            step.wait()
            dve.tensor_copy(zc[:, :], feat[:, 0:S]).then_inc(zc_ready, 1)
            keep_v2(0, 0)
            mix_q(0)
            mix_k(0, 0)
            maxima2(0, FIRST_USE)

            def row2(b, routes):
                for g in range(G2):
                    m, other = b * G2 + g, 1 - g
                    for j in range(4):
                        n, use = b * H2 + 4 * g + j, 4 * (4 * g + j)
                        dve.wait_ge(qb_done, 4 + n + 1)
                        keep_max(slice(32 * j, 32 * j + NT), pm, qb[j], n, max2_turned, max2_kept)
                        if j == 1:
                            norm_o(m, other)
                        maxima2(n + 1, use)
                        if j == 1:
                            keep_v2(m + 1, other)
                        if j == 3 and g == 0:
                            add_bias(b)
                        if j == 3 and g == 1:
                            gate_start(b)
                        if j == 0 and g == 0 and routes:
                            route(b)
                        if j == 0 and g == 1:
                            norm_u_roots(b)
                        if j == 1:
                            mix_q(m + 1)
                        if j == 1 and g == 0 and routes:
                            label(b)
                        if j == 1 and g == 1:
                            norm_u_end(b)
                        if j == 2:
                            mix_k(m + 1, other)
                        if j == 3 and g == 0:
                            dve.tensor_copy(zres[:, :], zc[:, :]).then_inc(zres_ready, 1)
                            dve.wait_ge(zres_ready, 1 + b + 1)
                            dve.tensor_copy(zc[:, :], feat_b(b + 1)).then_inc(zc_ready, 1)
                            norm_u(b)
                        if j == 3 and g == 1:
                            gate_end(b)

            row2(0, False)
            row2(1, False)
            with dve.Fori(2, B) as b:
                step.loop(b - 2, G2 + LN_STEPS + 1 + 4 + 4)
                row2(b, True)
                step.end(B - 2)
            route(B)
            label(B)
            norm_o(B * G2, 1)
            add_bias(B)
            norm_u(B)
            norm_u_roots(B)
            norm_u_end(B)
            gate_start(B)
            gate_end(B)
            route(B + 1)
            dve.wait_ge(rank_kept, B)
            dve.tensor_copy(runs_i[:, :], runs[0:1, :]).then_inc(counted, 1)
            label(B + 1)

            def one(a, n, w=NE):
                return cst[0:1, a:a + n * w].rearrange("p (i e) -> p i e", e=w)

            def done(ins):
                step.did(ins)
                step.wait()

            done(dve.tensor_tensor(cnt[:, :], runs[0:1, :], cst[0:1, C_REGION:C_REGION + NE], ALU.subtract))
            done(dve.tensor_tensor(more[:, :, :], cnt[:, :].unsqueeze(2).broadcast_to([1, NE, KT]), one(C_TILES, NE, KT), ALU.is_gt))
            done(dve.tensor_reduce(ntile[:, :], more[:, :, :], AX.X, ALU.add))
            done(dve.tensor_tensor(tri[:, :, :], ntile[:, :].unsqueeze(1).broadcast_to([1, NE, NE]), one(C_TRI, NE), ALU.mult))
            done(dve.tensor_reduce(upto[:, :], tri[:, :, :], AX.X, ALU.add))
            done(dve.tensor_tensor(past[:, :, :], one(C_WHICH, MT), upto[:, :].unsqueeze(1).broadcast_to([1, MT, NE]), ALU.is_ge))
            done(dve.tensor_reduce(whose[:, :], past[:, :, :], AX.X, ALU.add))
            done(dve.tensor_tensor(past_n[:, :, :], past[:, :, :], ntile[:, :].unsqueeze(1).broadcast_to([1, MT, NE]), ALU.mult))
            done(dve.tensor_reduce(before[:, :], past_n[:, :, :], AX.X, ALU.add))
            done(dve.scalar_tensor_tensor(out=before[:, :], in0=before[:, :], scalar=-float(TR), in1=cst[0:1, C_START:C_START + MT], op0=ALU.mult, op1=ALU.add))
            done(dve.scalar_tensor_tensor(out=before[:, :], in0=whose[:, :], scalar=float(CAP), in1=before[:, :], op0=ALU.mult, op1=ALU.add))
            done(dve.tensor_scalar(table[:, 0, :], before[:, :], float(NE * CAP), None, ALU.min))
            dve.tensor_scalar(table[:, 1, :], whose[:, :], float(NE - 1), 128.0, ALU.min, ALU.mult).then_inc(table_made, 1)

            def keep_x(i, k):
                dve.wait_ge(xt_made, i + 1)
                dve.tensor_copy(xf[k % 2][:, :], (px, py)[k % 2][:, 0:TR]).then_inc(xt_kept, 1)

            def finish(i, k, p):
                dve.wait_ge(y_moe_made, 2 + i + 1)
                stored(dve, k, p)
                dve.tensor_tensor(y[k % 2][:, :, :], po[k % 2][:, 0:TC * D].rearrange("p (t n) -> p t n", t=TC),
                                  we[k][:, M_B2:M_B2 + D].unsqueeze(1).broadcast_to([128, TC, D]), ALU.add).then_inc(y_moe_used, 1)
                dve.wait_ge(y_moe_used, 2 + i + 1)
                step.did(dve.tensor_tensor(y[k % 2][:, :, :], y[k % 2][:, :, :], xr[k][:, :, 2 * D:2 * D + 1].broadcast_to([128, TC, D]), ALU.mult))
                step.wait()
                dve.tensor_tensor(y[k % 2][:, :, :], y[k % 2][:, :, :], xr[k][:, :, D:2 * D], ALU.add).then_inc(y_done, 1)

            def tile(i, k, p):
                keep_x(i + 2, (k + 2) % AHEAD)
                finish(i, k, p)

            keep_x(0, 0)
            keep_x(1, 1)
            for k in range(AHEAD):
                tile(k, k, k // 2)
            by_tile(dve, tile, AHEAD, MT - 2, step, 1)
            for i in (MT - 2, MT - 1):
                finish(i, i % AHEAD, i // 2)

        @block.gpsimd
        def _(pool):
            step = Steps(pool, pool_step)
            pool.sem_inc(qb_done, 4)

            def fill(dst, value):
                step.wait()
                hold(pool)
                step.did(pool.memset(dst, value))

            for k in range(2):
                fill(yb[k][E1:E1 + 32, :].bitcast(F32), 1.0)
            fill(feat[:, B * S:(B + 1) * S], 0.0)
            fill(val[:, :, :, D:D + 1], 1.0)
            step.wait()
            pool.sem_inc(ones_set, 1)
            for j in range(4):
                fill(qa[j][:, :].bitcast(F32), 0.0)
                fill(qb[j][:, :].bitcast(F32), 0.0)
            fill(o_tok[:, :, :], 0.0)
            fill(zres[:, :], 0.0)
            fill(picks[:, :, :], 0.0)
            fill(val2[:, :, :, :], 1.0)
            step.wait()
            pool.sem_inc(zeroed, 1)
            pads = [[(0, offset(h)), (offset(h) + S, (offset(h) + S + 127) // 128 * 128)] for h in range(H1)]
            with pool.Fori(0, B) as b:
                step.loop(b, sum(hi > lo for h in range(H1) for lo, hi in pads[h]))
                for h in range(H1):
                    pool.wait_ge(max_turned, b * H1 + h + 1)
                    hold(pool)
                    for lo, hi in pads[h]:
                        if hi > lo:
                            fill(prob[h % 2][:, :, lo:hi], 0.0)
                    step.wait()
                    pool.sem_inc(pads_zero, 1)
                step.end(B)
            pool.wait_ge(z2_kept, 1 + B)

            def split_z(b):
                hold(pool)
                step.did(pool.tensor_copy(zc_hi[:, :], feat_b(b)))
                step.wait()
                hold(pool)
                pool.tensor_tensor(zc_lo[:, :], feat_b(b), zc_hi[:, :].bitcast(F32), ALU.subtract).then_inc(z2_split, 1)
                pool.wait_ge(z2_split, b + 1)

            def keep_qb(m, j):
                rows_j = slice(32 * j, 32 * j + 32)
                pool.wait_ge(q_hi_done, m + 1)
                pool.wait_ge(st2_made, m * 8 + 2 * j + 2)
                hold(pool)
                pool.tensor_copy(qb[j][rows_j, :], q_hi[rows_j, :].bitcast(F32)).then_inc(qb_done, 1)
                pool.wait_ge(qb_done, 4 + m * 4 + j + 1)

            def scale_t(b):
                pool.wait_ge(ln3_done, b + 1)
                hold(pool)
                wide = [rows[:, c:c + D].unsqueeze(1).broadcast_to([R, NT, D]) for c in (Q_G, Q_BETA)]
                step.did(pool.tensor_tensor(ln_out[:, :, :], ln_out[:, :, :], wide[0], ALU.mult))
                step.wait()
                pool.tensor_tensor(pay[:, :, 0:D], ln_out[:, :, :], wide[1], ALU.add).then_inc(t_ready, 1)
                pool.wait_ge(t_ready, b + 1)

            def keep_res(b):
                hold(pool)
                pool.tensor_copy(pay[:, :, D:2 * D], resid[:, bass.ds(b - 1, 1), :].rearrange("p a (t n) -> p (a t) n", t=NT)).then_inc(pay_res, 1)
                pool.wait_ge(pay_res, b)

            def send(b):
                pool.wait_ge(placed, b - 1)
                pool.wait_ge(t_turned, b)
                hold(pool)
                for t in range(NT):
                    pool.indirect_dma_start(routed, bass.IndirectOffsetOnAxis(ap=place_i[:, t:t + 1], axis=0),
                                            pay[:, t, :], None).then_inc(d_routed, 16)
                pool.wait_ge(d_routed, (b - 1) * 16 * NT)

            pool.wait_ge(d_rows, 16)
            split_z(0)
            for j in range(3):
                keep_qb(0, j)

            def row2(b, routes, real):
                for g in range(G2):
                    m = b * G2 + g
                    keep_qb(m, 3)
                    if g == 0 and routes:
                        send(b)
                    if g == 1:
                        scale_t(b)
                        if real:
                            keep_res(b)
                    keep_qb(m + 1, 0)
                    keep_qb(m + 1, 1)
                    if g == 0:
                        pool.wait_ge(k_made, m + 2)
                        split_z(b + 1)
                    keep_qb(m + 1, 2)

            row2(0, False, False)
            row2(1, False, True)
            with pool.Fori(2, B) as b:
                step.loop(b - 2, 2)
                row2(b, True, True)
                step.end(B - 2)
            send(B)
            scale_t(B)
            keep_res(B)
            send(B + 1)

            def store(i, k, p):
                pool.wait_ge(y_done, i + 1)
                stored(pool, k, p)
                hold(pool)
                for t in range(TC):
                    pool.indirect_dma_start(out_rows, bass.IndirectOffsetOnAxis(ap=xr[k][:, t, 2 * D + 1:2 * D + 2].bitcast(I32), axis=0),
                                            y[k % 2][:, t, :], None, bounds_check=N - 1, oob_is_err=False).then_inc(d_out[k % 2], 16)

            for k in range(AHEAD):
                store(k, k, k // 2)
            by_tile(pool, store, AHEAD)


_IN = ("xt", "conv_w", "att1_w", "att2_w", "rows_w", "moe_w", "pads", "consts")


def kernel(**inputs):
    import concourse.bacc as _bacc
    from concourse.bass_utils import run_bass_kernel_spmd as _run

    a = {k: np.asarray(v) for k, v in inputs.items()}
    f32 = np.float32

    def wide(w, n):
        full = np.zeros((128, w.shape[1]), f32)
        full[:n] = w
        return full

    arrays = {}
    arrays["xt"] = np.zeros((KIN, B * T), f32)
    arrays["xt"][:FIN] = a["x"].transpose(2, 0, 1).reshape(FIN, B * T)
    w = a["L0_tok_W"].reshape(D, TAPS, FIN).transpose(2, 1, 0).reshape(FIN, TAPS * D)
    arrays["conv_w"] = np.concatenate([wide(w, FIN), a["L0_tok_b"][:, None], a["L0_tok_gamma"][:, None],
                                       a["L0_tok_beta"][:, None]], axis=1)

    def twice(w):
        w = w.transpose(1, 0, 2)
        return np.concatenate([w, w], axis=2).reshape(D, -1)

    arrays["att1_w"] = np.concatenate([
        twice(a["L0_attn_Wk"]), twice(a["L0_attn_Wq"]), a["L0_attn_Wv"].transpose(1, 0, 2).reshape(D, -1),
        a["L0_attn_Wlt"].reshape(H1, 128, D).transpose(1, 0, 2).reshape(128, -1)], axis=1)

    cols = np.array([[16 * (4 * g + p // 32) + p % 16 for p in range(128)] for g in range(G2)])
    arrays["att2_w"] = np.concatenate([
        a["L0_ffn_Wq"][:, cols.reshape(-1)], a["L0_ffn_Wk"][:, cols.reshape(-1)], a["L0_ffn_Wv"], a["L0_ffn_Wo"],
        a["L0_ffn_gate_W"], a["L0_ffn_bq"][cols].T, a["L0_ffn_bk"][cols].T], axis=1)
    arrays["rows_w"] = np.ascontiguousarray(np.broadcast_to(np.concatenate([
        a["L0_ffn_bv"], a["L0_ffn_bo"], a["L0_ffn_ln1_g"], a["L0_ffn_ln1_b"], a["L0_ffn_gate_b"]]), (R, Q_END)))
    arrays["moe_w"] = np.concatenate([
        a["L0_ffn_W1"], a["L0_ffn_W2"].reshape(NE, NC, 128, D).transpose(0, 2, 1, 3).reshape(NE, 128, -1),
        a["L0_ffn_b1"].reshape(NE, NC, 128).transpose(0, 2, 1),
        np.broadcast_to(a["L0_ffn_b2"][:, None, :], (NE, 128, D))], axis=2).reshape(NE * 128, M_END)
    pads = np.zeros((128, TC, PAY), f32)
    pads.view(np.int32)[:, :, PAY - 1] = NOBODY
    arrays["pads"] = pads.reshape(128, TC * PAY)

    p = np.arange(128)
    consts = np.zeros((128, C_END), f32)
    consts[:, C_ID:C_ID + 128] = np.eye(128)
    for t in range(NT):
        consts[p % 32 == t, C_BLK + t * R:C_BLK + (t + 1) * R] = -1.0
    consts[:, C_MHI] = p % 32 < 16
    consts[:, C_MLO] = p % 32 >= 16
    consts[:, C_ONE4] = p % 32 < NT
    consts[:, C_NLO] = -(p % 32 >= 16).astype(f32)
    consts[:, C_REV:C_UP] = np.tile(NE - np.arange(NE), NT)
    consts[:R, C_UP:C_ONES] = np.triu(np.ones((R, R)), 1)
    consts[:, C_ONES:C_TOKEN] = 1.0
    consts[:R, C_TOKEN:C_REGION] = p[:R, None] + R * np.arange(NT)
    consts[:, C_REGION:C_TILES] = CAP * np.arange(NE)
    consts[:, C_TILES:C_TRI] = np.tile(TR * np.arange(KT), NE)
    consts[:, C_TRI:C_WHICH] = np.tril(np.ones((NE, NE))).reshape(-1)
    consts[:, C_WHICH:C_START] = np.repeat(np.arange(MT), NE)
    consts[:, C_START:C_END] = TR * np.arange(MT)
    arrays["consts"] = consts

    nc = _bacc.Bacc("TRN2", target_bir_lowering=False, num_devices=1)
    arrays = {f"in_{k}": np.ascontiguousarray(v) for k, v in arrays.items()}
    args = [nc.dram_tensor(f"in_{k}", arrays[f"in_{k}"].shape, F32, kind="ExternalInput").ap() for k in _IN]
    o = nc.dram_tensor("out", (B, S, D), F32, kind="ExternalOutput").ap()
    routed = nc.dram_tensor("routed", (NE * CAP + TR, PAY), F32, kind="Internal").ap()
    tower(nc, *args, routed, o)
    r = _run(nc, [arrays], core_ids=[0])
    return r.results[0]["out"]
```
